# Optimizing a Trainium2 kernel written in Bass

```python
import numpy as np
import jax
import jax.numpy as jnp

def _softmax(x, axis=-1):
    return jax.nn.softmax(x, axis=axis)

def _gelu(x):
    return jax.nn.gelu(x, approximate=True)

def _silu(x):
    return jax.nn.silu(x)

def _sigmoid(x):
    return jax.nn.sigmoid(x)

def _layernorm(x, axis=-1, eps=1e-05):
    m = jnp.mean(x, axis=axis, keepdims=True)
    v = jnp.var(x, axis=axis, keepdims=True)
    return (x - m) / jnp.sqrt(v + eps)

def _scatter_add(tgt, idx, src, axis=0):
    return tgt.at[idx].add(src)

def _segment_sum(src, seg, n):
    return jax.ops.segment_sum(src, seg, n)
kernel_name = 'mk_perceiver_d2_seqx_r8_9daa45'

def setup_inputs(seed: int=0):
    np.random.seed(seed)
    _w = jnp.asarray

    def _rec_inputs():
        import jax
        import jax.numpy as jnp
        _rk = jax.random.key(seed)
        x = 7.22e-05 + 1 * jax.random.normal(jax.random.fold_in(_rk, 1), (32, 64, 128), jnp.float32)
        _lenS = 64 - jax.random.randint(jax.random.fold_in(_rk, 7), (32,), 0, max(1, 64 // 4) + 1, jnp.int32)
        _lenS2 = 1601 - jax.random.randint(jax.random.fold_in(_rk, 8), (32,), 0, max(1, 1601 // 4) + 1, jnp.int32)
        _ctx_1024P = jax.random.normal(jax.random.fold_in(_rk, 11), (32, 16, 128), jnp.float32)
        _ctx_1024c = jax.random.dirichlet(jax.random.fold_in(_rk, 511), 0.3 * jnp.ones((16,), jnp.float32), (32, 1601))
        _ctx_1024t = jnp.einsum('bsk,bkd->bsd', _ctx_1024c, _ctx_1024P)
        _ctx_1024t = _ctx_1024t * jax.lax.rsqrt(jnp.mean(jnp.square(_ctx_1024t)) + 1e-12) * 0.953939
        ctx_1024 = 4.13588e-05 + 0.999923 * (_ctx_1024t + 0.3 * jax.random.normal(jax.random.fold_in(_rk, 611), (32, 1601, 128), jnp.float32))
        _validS = jnp.arange(64)[None, :] < _lenS[:, None]
        _validS2 = jnp.arange(1601)[None, :] < _lenS2[:, None]
        _causal = jnp.tril(jnp.ones((64, 64), dtype=bool))
        mask_BxS2_ik0 = jnp.where(jnp.broadcast_to(_validS2[:, :], (32, 1601)), 0, 1).astype(jnp.int32)
        return (x, ctx_1024, mask_BxS2_ik0)
    x, ctx_1024, mask_BxS2_ik0 = _rec_inputs()

    def _L0_xattn_setup():
        import jax, jax.numpy as jnp
        import numpy as np
        EMB_DIM = 128
        NUM_HEADS = 16
        HEAD_DIM = EMB_DIM // NUM_HEADS
        B, S_Q, S_KV = (4, 256, 256)
        key = jax.random.key(seed)
        ks = jax.random.split(key, 12)
        s = EMB_DIM ** (-0.5)
        inp = {'q': jax.random.normal(ks[0], (B, S_Q, EMB_DIM), jnp.float32), 'k': jax.random.normal(ks[1], (B, S_KV, EMB_DIM), jnp.float32), 'v': jax.random.normal(ks[2], (B, S_KV, EMB_DIM), jnp.float32), 'mask': jax.random.randint(ks[3], (B, S_KV), 0, 2, jnp.int32), 'Wq': jax.random.normal(ks[4], (EMB_DIM, EMB_DIM), jnp.float32) * s, 'bq': jnp.zeros((EMB_DIM,), jnp.float32), 'Wk': jax.random.normal(ks[5], (EMB_DIM, EMB_DIM), jnp.float32) * s, 'bk': jnp.zeros((EMB_DIM,), jnp.float32), 'Wv': jax.random.normal(ks[6], (EMB_DIM, EMB_DIM), jnp.float32) * s, 'bv': jnp.zeros((EMB_DIM,), jnp.float32), 'Wo': jax.random.normal(ks[7], (EMB_DIM, EMB_DIM), jnp.float32) * s, 'bo': jnp.zeros((EMB_DIM,), jnp.float32)}
        return inp
    _L0_xattn_all = _L0_xattn_setup()
    _L0_xattn_in = {k: v for k, v in _L0_xattn_all.items() if k in ('Wq', 'bq', 'Wk', 'bk', 'Wv', 'bv', 'Wo', 'bo')}
    del _L0_xattn_all

    def _L0_attn_setup():
        import jax, jax.numpy as jnp
        import numpy as np
        from jax.scipy.linalg import solve_triangular
        B, T, D = (2, 512, 128)
        HEAD_DIM = 128
        CHUNK = 64

        def _forward(out, W_write, W_read, W_alpha, W_beta, A_log, dt_bias):
            Bs, Ts, Ds = out.shape
            d, C = (HEAD_DIM, CHUNK)
            H = Ds // d
            x = out.astype(jnp.float32)
            rk = x.reshape(Bs, Ts, H, d)
            rk = rk / jnp.maximum(jnp.linalg.norm(rk, axis=-1, keepdims=True), 1e-12)
            rk = jnp.swapaxes(rk, 1, 2)
            wk = jnp.pad(rk[:, :, :-1], ((0, 0), (0, 0), (1, 0), (0, 0)))
            v = jnp.einsum('btd,ed->bte', x, W_write).reshape(Bs, Ts, H, d)
            v = jnp.swapaxes(v, 1, 2)
            beta = jax.nn.sigmoid(jnp.einsum('btd,hd->bth', x, W_beta))
            beta = jnp.swapaxes(beta, 1, 2)[..., None]
            log_decay = -jnp.exp(A_log)[None, None, :] * jax.nn.softplus(jnp.einsum('btd,hd->bth', x, W_alpha) + dt_bias)
            log_decay = jnp.swapaxes(log_decay, 1, 2)
            v_scaled = v * beta
            wk_scaled = wk * beta
            pad = -Ts % C
            if pad:
                p4 = ((0, 0), (0, 0), (0, pad), (0, 0))
                rk = jnp.pad(rk, p4)
                wk = jnp.pad(wk, p4)
                v_scaled = jnp.pad(v_scaled, p4)
                wk_scaled = jnp.pad(wk_scaled, p4)
                log_decay = jnp.pad(log_decay, ((0, 0), (0, 0), (0, pad)))
            Tp = Ts + pad
            N = Tp // C
            chunk = lambda a: a.reshape(Bs, H, N, C, d)
            rk, wk, v_scaled, wk_scaled = map(chunk, (rk, wk, v_scaled, wk_scaled))
            log_decay = log_decay.reshape(Bs, H, N, C)
            cum = jnp.cumsum(log_decay, -1)
            L_mask = jnp.tril(jnp.exp(jnp.tril(cum[..., :, None] - cum[..., None, :])))
            decay_exp = jnp.exp(cum)[..., None]
            chunk_end_decay = jnp.exp(cum[..., -1])
            M = jnp.tril(-(wk_scaled @ jnp.swapaxes(wk, -1, -2)) * L_mask, -1)
            eye = jnp.eye(C, dtype=x.dtype)
            A = solve_triangular(eye - M, jnp.broadcast_to(eye, M.shape), lower=True, unit_diagonal=True)
            intra = jnp.tril(rk @ jnp.swapaxes(wk, -1, -2) * L_mask, -1)
            rk_decay = rk * decay_exp
            tail_decay = jnp.exp(cum[..., -1:] - cum)[..., None]
            wk_pos = jnp.swapaxes(wk * tail_decay, -1, -2)
            wk_scaled_dec = wk_scaled * decay_exp
            toN = lambda a: jnp.moveaxis(a, 2, 0)

            def step(S, inp):
                A_i, vsc_i, wkd_i, rkd_i, intra_i, wkp_i, ced_i = inp
                v_new = A_i @ vsc_i - A_i @ wkd_i @ S
                o_i = rkd_i @ S + intra_i @ v_new
                S = ced_i[..., None, None] * S + wkp_i @ v_new
                return (S, o_i)
            S0 = jnp.zeros((Bs, H, d, d), x.dtype)
            _, o = jax.lax.scan(step, S0, (toN(A), toN(v_scaled), toN(wk_scaled_dec), toN(rk_decay), toN(intra), toN(wk_pos), jnp.moveaxis(chunk_end_decay, 2, 0)))
            o = jnp.moveaxis(o, 0, 2).reshape(Bs, H, Tp, d)
            o = jnp.swapaxes(o, 1, 2).reshape(Bs, Tp, Ds)[:, :Ts]
            return out + jnp.einsum('btd,ed->bte', o, W_read).astype(out.dtype)
        key = jax.random.key(seed)
        ks = jax.random.split(key, 7)
        H = D // HEAD_DIM
        out = jax.random.normal(ks[0], (B, T, D), dtype=jnp.float32)
        scale = D ** (-0.5)
        W_write = jax.random.normal(ks[1], (D, D), jnp.float32) * scale
        W_read = jax.random.normal(ks[2], (D, D), jnp.float32) * scale
        W_alpha = jax.random.normal(ks[3], (H, D), jnp.float32) * scale
        W_beta = jax.random.normal(ks[4], (H, D), jnp.float32) * scale
        A_log = jnp.log(jax.random.uniform(ks[5], (H,), jnp.float32, 0.05, 16.0))
        dt_bias = jnp.ones((H,), jnp.float32)
        return {'out': out, 'W_write': W_write, 'W_read': W_read, 'W_alpha': W_alpha, 'W_beta': W_beta, 'A_log': A_log, 'dt_bias': dt_bias}
    _L0_attn_all = _L0_attn_setup()
    _L0_attn_in = {k: v for k, v in _L0_attn_all.items() if k in ('W_write', 'W_read', 'W_alpha', 'W_beta', 'A_log', 'dt_bias')}
    del _L0_attn_all

    def _L0_ffn_setup():
        import jax, jax.numpy as jnp
        import numpy as np
        D_MODEL = 128
        N_EXPERTS = 8
        TOP_K = 2
        key = jax.random.key(seed)
        k1, k2, k3, k4 = jax.random.split(key, 4)
        B, S, D, E = (4, 256, D_MODEL, N_EXPERTS)
        dff = 4 * D
        lim = float(np.sqrt(6.0 / (D + dff)))
        return {'x': jax.random.normal(k1, (B, S, D), dtype=jnp.float32), 'router_w': jax.random.normal(k2, (D, E), dtype=jnp.float32) * (1.0 / np.sqrt(D)), 'router_b': jnp.zeros((E,), dtype=jnp.float32), 'expert_up': jax.random.uniform(k3, (E, dff, D), dtype=jnp.float32, minval=-lim, maxval=lim), 'expert_down': jax.random.uniform(k4, (E, D, dff), dtype=jnp.float32, minval=-lim, maxval=lim)}
    _L0_ffn_all = _L0_ffn_setup()
    _L0_ffn_in = {k: v for k, v in _L0_ffn_all.items() if k in ('router_w', 'router_b', 'expert_up', 'expert_down')}
    del _L0_ffn_all

    def _L1_xattn_setup():
        import jax, jax.numpy as jnp
        import numpy as np
        D_MODEL = 128
        D_HEAD = 64
        NHEADS = 8
        IN_DIM = D_HEAD * NHEADS
        EPS = 1e-05

        def layernorm(x, g, b):
            mu = jnp.mean(x, axis=-1, keepdims=True)
            var = jnp.var(x, axis=-1, keepdims=True)
            return (x - mu) * jax.lax.rsqrt(var + EPS) * g + b
        key = jax.random.key(seed)
        ks = jax.random.split(key, 8)
        B, M, L = (4, 1024, 64)
        x = jax.random.normal(ks[0], (B, M, D_MODEL), dtype=jnp.float32)
        latents = jax.random.normal(ks[1], (B, L, D_MODEL), dtype=jnp.float32)
        s = 1.0 / np.sqrt(D_MODEL)
        Wq = jax.random.normal(ks[2], (D_MODEL, IN_DIM), dtype=jnp.float32) * s
        Wkv = jax.random.normal(ks[3], (D_MODEL, 2 * IN_DIM), dtype=jnp.float32) * s
        Wout = jax.random.normal(ks[4], (IN_DIM, D_MODEL), dtype=jnp.float32) * (1.0 / np.sqrt(IN_DIM))
        gm = jnp.ones((D_MODEL,), jnp.float32)
        bm = jnp.zeros((D_MODEL,), jnp.float32)
        gl = jnp.ones((D_MODEL,), jnp.float32)
        bl = jnp.zeros((D_MODEL,), jnp.float32)
        return {'x': x, 'latents': latents, 'Wq': Wq, 'Wkv': Wkv, 'Wout': Wout, 'gm': gm, 'bm': bm, 'gl': gl, 'bl': bl}
    _L1_xattn_all = _L1_xattn_setup()
    _L1_xattn_in = {k: v for k, v in _L1_xattn_all.items() if k in ('Wq', 'Wkv', 'Wout', 'gm', 'bm', 'gl', 'bl')}
    del _L1_xattn_all

    def _L1_attn_setup():
        import jax, jax.numpy as jnp
        import numpy as np
        import math
        B, L, D_MODEL = (8, 256, 128)
        D_INNER, D_SSM = (256, 128)
        KEY_DIM, VALUE_DIM, H = (96, 192, 4)
        DK, DV = (KEY_DIM // H, VALUE_DIM // H)
        D_CONV = 4
        EPS = 1e-05

        def _dwconv(x, w, b):
            y = jax.lax.conv_general_dilated(x, w, window_strides=(1,), padding=[(1, 2)], dimension_numbers=('NCH', 'OIH', 'NCH'), feature_group_count=x.shape[1])
            return y + b[None, :, None]

        def _l2norm(x):
            return x * jax.lax.rsqrt(jnp.sum(x * x, axis=-1, keepdims=True) + 1e-06)

        def _gated_delta_rule(q, k, v, beta, gk):
            qT = jnp.moveaxis(q, 2, 0)
            kT = jnp.moveaxis(k, 2, 0)
            vT = jnp.moveaxis(v, 2, 0)
            bT = jnp.moveaxis(beta, 2, 0)
            gT = jnp.moveaxis(gk, 2, 0)
            S0 = jnp.zeros((q.shape[0], q.shape[1], q.shape[3], v.shape[3]), q.dtype)

            def step(S, inp):
                qt, kt, vt, bt, gt = inp
                S = S * jnp.exp(gt)[..., None, None]
                u = bt[..., None] * (vt - jnp.einsum('bhk,bhkv->bhv', kt, S))
                S = S + jnp.einsum('bhk,bhv->bhkv', kt, u)
                ot = jnp.einsum('bhk,bhkv->bhv', qt, S)
                return (S, ot)
            _, o = jax.lax.scan(step, S0, (qT, kT, vT, bT, gT))
            return jnp.moveaxis(o, 0, 2)
        key = jax.random.key(seed)
        ks = jax.random.split(key, 20)

        def w(k, shape, fan_in):
            return jax.random.normal(k, shape, jnp.float32) / np.sqrt(fan_in)
        dt = jnp.exp(jax.random.uniform(ks[14], (H,)) * (math.log(0.1) - math.log(0.001)) + math.log(0.001))
        dt = jnp.clip(dt, 0.0001)
        dt_bias = dt + jnp.log(-jnp.expm1(-dt))
        A = jax.random.uniform(ks[13], (H,), minval=0.5, maxval=16.0)
        return {'x': jax.random.normal(ks[0], (B, L, D_MODEL), jnp.float32), 'W_in': w(ks[1], (D_MODEL, D_INNER), D_MODEL), 'conv_x_w': w(ks[2], (D_SSM, 1, D_CONV), D_CONV), 'conv_x_b': jnp.zeros((D_SSM,), jnp.float32), 'conv_z_w': w(ks[3], (D_SSM, 1, D_CONV), D_CONV), 'conv_z_b': jnp.zeros((D_SSM,), jnp.float32), 'W_q': w(ks[4], (D_SSM, KEY_DIM), D_SSM), 'W_k': w(ks[5], (D_SSM, KEY_DIM), D_SSM), 'W_v': w(ks[6], (D_SSM, VALUE_DIM), D_SSM), 'W_g': w(ks[7], (D_SSM, VALUE_DIM), D_SSM), 'W_gk': w(ks[8], (D_SSM, H), D_SSM), 'W_b': w(ks[9], (D_SSM, H), D_SSM), 'b_b': jnp.zeros((H,), jnp.float32), 'A_log': jnp.log(A), 'dt_bias': dt_bias, 'g_norm_w': jnp.ones((DV,), jnp.float32), 'W_so': w(ks[10], (VALUE_DIM, D_SSM), VALUE_DIM), 'W_out': w(ks[11], (D_INNER, D_MODEL), D_INNER)}
    _L1_attn_all = _L1_attn_setup()
    _L1_attn_in = {k: v for k, v in _L1_attn_all.items() if k in ('W_in', 'conv_x_w', 'conv_x_b', 'conv_z_w', 'conv_z_b', 'W_q', 'W_k', 'W_v', 'W_g', 'W_gk', 'W_b', 'b_b', 'A_log', 'dt_bias', 'g_norm_w', 'W_so', 'W_out')}
    del _L1_attn_all

    def _L1_ffn_setup():
        import jax, jax.numpy as jnp
        import numpy as np
        EPS = 1e-05
        NUM_HEADS = 16
        NUM_KV_HEADS = 4
        NUM_EXPERTS = 8
        TOP_K = 2

        def _layernorm(x, w, b):
            mu = jnp.mean(x, axis=-1, keepdims=True)
            var = jnp.mean((x - mu) ** 2, axis=-1, keepdims=True)
            return (x - mu) * jax.lax.rsqrt(var + EPS) * w + b
        key = jax.random.key(seed)
        ks = jax.random.split(key, 8)
        S, B, H = (128, 4, 128)
        F = 256
        hd = H // NUM_HEADS
        qkv_out = (NUM_HEADS + 2 * NUM_KV_HEADS) * hd
        w_scale = 0.02
        return {'hidden_states': jax.random.normal(ks[0], (S, B, H), jnp.float32), 'ln1_weight': jnp.ones((H,), jnp.float32), 'ln1_bias': jnp.zeros((H,), jnp.float32), 'ln2_weight': jnp.ones((H,), jnp.float32), 'ln2_bias': jnp.zeros((H,), jnp.float32), 'qkv_weight': jax.random.normal(ks[1], (qkv_out, H), jnp.float32) * w_scale, 'proj_weight': jax.random.normal(ks[2], (H, H), jnp.float32) * w_scale, 'router_weight': jax.random.normal(ks[3], (NUM_EXPERTS, H), jnp.float32) * w_scale, 'moe_w1': jax.random.normal(ks[4], (NUM_EXPERTS, H, F), jnp.float32) * w_scale, 'moe_w2': jax.random.normal(ks[5], (NUM_EXPERTS, F, H), jnp.float32) * w_scale}
    _L1_ffn_all = _L1_ffn_setup()
    _L1_ffn_in = {k: v for k, v in _L1_ffn_all.items() if k in ('ln1_weight', 'ln1_bias', 'ln2_weight', 'ln2_bias', 'qkv_weight', 'proj_weight', 'router_weight', 'moe_w1', 'moe_w2')}
    del _L1_ffn_all
    return {'x': x, 'ctx_1024': ctx_1024, 'mask_BxS2_ik0': mask_BxS2_ik0, 'L0_xattn_Wq': _L0_xattn_in['Wq'], 'L0_xattn_bq': _L0_xattn_in['bq'], 'L0_xattn_Wk': _L0_xattn_in['Wk'], 'L0_xattn_bk': _L0_xattn_in['bk'], 'L0_xattn_Wv': _L0_xattn_in['Wv'], 'L0_xattn_bv': _L0_xattn_in['bv'], 'L0_xattn_Wo': _L0_xattn_in['Wo'], 'L0_xattn_bo': _L0_xattn_in['bo'], 'L0_attn_W_write': _L0_attn_in['W_write'], 'L0_attn_W_read': _L0_attn_in['W_read'], 'L0_attn_W_alpha': _L0_attn_in['W_alpha'], 'L0_attn_W_beta': _L0_attn_in['W_beta'], 'L0_attn_A_log': _L0_attn_in['A_log'], 'L0_attn_dt_bias': _L0_attn_in['dt_bias'], 'L0_ffn_router_w': _L0_ffn_in['router_w'], 'L0_ffn_router_b': _L0_ffn_in['router_b'], 'L0_ffn_expert_up': _L0_ffn_in['expert_up'], 'L0_ffn_expert_down': _L0_ffn_in['expert_down'], 'L1_xattn_Wq': _L1_xattn_in['Wq'], 'L1_xattn_Wkv': _L1_xattn_in['Wkv'], 'L1_xattn_Wout': _L1_xattn_in['Wout'], 'L1_xattn_gm': _L1_xattn_in['gm'], 'L1_xattn_bm': _L1_xattn_in['bm'], 'L1_xattn_gl': _L1_xattn_in['gl'], 'L1_xattn_bl': _L1_xattn_in['bl'], 'L1_attn_W_in': _L1_attn_in['W_in'], 'L1_attn_conv_x_w': _L1_attn_in['conv_x_w'], 'L1_attn_conv_x_b': _L1_attn_in['conv_x_b'], 'L1_attn_conv_z_w': _L1_attn_in['conv_z_w'], 'L1_attn_conv_z_b': _L1_attn_in['conv_z_b'], 'L1_attn_W_q': _L1_attn_in['W_q'], 'L1_attn_W_k': _L1_attn_in['W_k'], 'L1_attn_W_v': _L1_attn_in['W_v'], 'L1_attn_W_g': _L1_attn_in['W_g'], 'L1_attn_W_gk': _L1_attn_in['W_gk'], 'L1_attn_W_b': _L1_attn_in['W_b'], 'L1_attn_b_b': _L1_attn_in['b_b'], 'L1_attn_A_log': _L1_attn_in['A_log'], 'L1_attn_dt_bias': _L1_attn_in['dt_bias'], 'L1_attn_g_norm_w': _L1_attn_in['g_norm_w'], 'L1_attn_W_so': _L1_attn_in['W_so'], 'L1_attn_W_out': _L1_attn_in['W_out'], 'L1_ffn_ln1_weight': _L1_ffn_in['ln1_weight'], 'L1_ffn_ln1_bias': _L1_ffn_in['ln1_bias'], 'L1_ffn_ln2_weight': _L1_ffn_in['ln2_weight'], 'L1_ffn_ln2_bias': _L1_ffn_in['ln2_bias'], 'L1_ffn_qkv_weight': _L1_ffn_in['qkv_weight'], 'L1_ffn_proj_weight': _L1_ffn_in['proj_weight'], 'L1_ffn_router_weight': _L1_ffn_in['router_weight'], 'L1_ffn_moe_w1': _L1_ffn_in['moe_w1'], 'L1_ffn_moe_w2': _L1_ffn_in['moe_w2']}

def reference(x, ctx_1024, mask_BxS2_ik0, L0_xattn_Wq, L0_xattn_bq, L0_xattn_Wk, L0_xattn_bk, L0_xattn_Wv, L0_xattn_bv, L0_xattn_Wo, L0_xattn_bo, L0_attn_W_write, L0_attn_W_read, L0_attn_W_alpha, L0_attn_W_beta, L0_attn_A_log, L0_attn_dt_bias, L0_ffn_router_w, L0_ffn_router_b, L0_ffn_expert_up, L0_ffn_expert_down, L1_xattn_Wq, L1_xattn_Wkv, L1_xattn_Wout, L1_xattn_gm, L1_xattn_bm, L1_xattn_gl, L1_xattn_bl, L1_attn_W_in, L1_attn_conv_x_w, L1_attn_conv_x_b, L1_attn_conv_z_w, L1_attn_conv_z_b, L1_attn_W_q, L1_attn_W_k, L1_attn_W_v, L1_attn_W_g, L1_attn_W_gk, L1_attn_W_b, L1_attn_b_b, L1_attn_A_log, L1_attn_dt_bias, L1_attn_g_norm_w, L1_attn_W_so, L1_attn_W_out, L1_ffn_ln1_weight, L1_ffn_ln1_bias, L1_ffn_ln2_weight, L1_ffn_ln2_bias, L1_ffn_qkv_weight, L1_ffn_proj_weight, L1_ffn_router_weight, L1_ffn_moe_w1, L1_ffn_moe_w2):
    import jax
    import jax.numpy as jnp

    def _L0_xattn_ref(q, k, v, mask, Wq, bq, Wk, bk, Wv, bv, Wo, bo):
        import jax, jax.numpy as jnp
        import numpy as np
        EMB_DIM = 128
        NUM_HEADS = 16
        HEAD_DIM = EMB_DIM // NUM_HEADS
        B, S_Q, S_KV = (4, 256, 256)
        Bsz, Sq, E = q.shape
        Skv = k.shape[1]
        H, D = (NUM_HEADS, HEAD_DIM)
        scale = D ** (-0.5)
        qh = (q @ Wq.T + bq).reshape(Bsz, Sq, H, D).transpose(0, 2, 1, 3)
        kh = (k @ Wk.T + bk).reshape(Bsz, Skv, H, D).transpose(0, 2, 1, 3)
        vh = (v @ Wv.T + bv).reshape(Bsz, Skv, H, D).transpose(0, 2, 1, 3)
        attn = jnp.einsum('bhqd,bhkd->bhqk', qh, kh) * scale
        valid = mask != 0
        all_invalid = ~jnp.any(valid, axis=-1, keepdims=True)
        safe = valid | all_invalid
        attn = jnp.where(safe[:, None, None, :], attn, -jnp.inf)
        attn = jax.nn.softmax(attn, axis=-1)
        attn = jnp.where(all_invalid.reshape(Bsz, 1, 1, 1), 0.0, attn)
        out = jnp.einsum('bhqk,bhkd->bhqd', attn, vh)
        out = out.transpose(0, 2, 1, 3).reshape(Bsz, Sq, E)
        return out @ Wo.T + bo

    def _L0_attn_ref(out, W_write, W_read, W_alpha, W_beta, A_log, dt_bias):
        import jax, jax.numpy as jnp
        import numpy as np
        from jax.scipy.linalg import solve_triangular
        B, T, D = (2, 512, 128)
        HEAD_DIM = 128
        CHUNK = 64

        def _forward(out, W_write, W_read, W_alpha, W_beta, A_log, dt_bias):
            Bs, Ts, Ds = out.shape
            d, C = (HEAD_DIM, CHUNK)
            H = Ds // d
            x = out.astype(jnp.float32)
            rk = x.reshape(Bs, Ts, H, d)
            rk = rk / jnp.maximum(jnp.linalg.norm(rk, axis=-1, keepdims=True), 1e-12)
            rk = jnp.swapaxes(rk, 1, 2)
            wk = jnp.pad(rk[:, :, :-1], ((0, 0), (0, 0), (1, 0), (0, 0)))
            v = jnp.einsum('btd,ed->bte', x, W_write).reshape(Bs, Ts, H, d)
            v = jnp.swapaxes(v, 1, 2)
            beta = jax.nn.sigmoid(jnp.einsum('btd,hd->bth', x, W_beta))
            beta = jnp.swapaxes(beta, 1, 2)[..., None]
            log_decay = -jnp.exp(A_log)[None, None, :] * jax.nn.softplus(jnp.einsum('btd,hd->bth', x, W_alpha) + dt_bias)
            log_decay = jnp.swapaxes(log_decay, 1, 2)
            v_scaled = v * beta
            wk_scaled = wk * beta
            pad = -Ts % C
            if pad:
                p4 = ((0, 0), (0, 0), (0, pad), (0, 0))
                rk = jnp.pad(rk, p4)
                wk = jnp.pad(wk, p4)
                v_scaled = jnp.pad(v_scaled, p4)
                wk_scaled = jnp.pad(wk_scaled, p4)
                log_decay = jnp.pad(log_decay, ((0, 0), (0, 0), (0, pad)))
            Tp = Ts + pad
            N = Tp // C
            chunk = lambda a: a.reshape(Bs, H, N, C, d)
            rk, wk, v_scaled, wk_scaled = map(chunk, (rk, wk, v_scaled, wk_scaled))
            log_decay = log_decay.reshape(Bs, H, N, C)
            cum = jnp.cumsum(log_decay, -1)
            L_mask = jnp.tril(jnp.exp(jnp.tril(cum[..., :, None] - cum[..., None, :])))
            decay_exp = jnp.exp(cum)[..., None]
            chunk_end_decay = jnp.exp(cum[..., -1])
            M = jnp.tril(-(wk_scaled @ jnp.swapaxes(wk, -1, -2)) * L_mask, -1)
            eye = jnp.eye(C, dtype=x.dtype)
            A = solve_triangular(eye - M, jnp.broadcast_to(eye, M.shape), lower=True, unit_diagonal=True)
            intra = jnp.tril(rk @ jnp.swapaxes(wk, -1, -2) * L_mask, -1)
            rk_decay = rk * decay_exp
            tail_decay = jnp.exp(cum[..., -1:] - cum)[..., None]
            wk_pos = jnp.swapaxes(wk * tail_decay, -1, -2)
            wk_scaled_dec = wk_scaled * decay_exp
            toN = lambda a: jnp.moveaxis(a, 2, 0)

            def step(S, inp):
                A_i, vsc_i, wkd_i, rkd_i, intra_i, wkp_i, ced_i = inp
                v_new = A_i @ vsc_i - A_i @ wkd_i @ S
                o_i = rkd_i @ S + intra_i @ v_new
                S = ced_i[..., None, None] * S + wkp_i @ v_new
                return (S, o_i)
            S0 = jnp.zeros((Bs, H, d, d), x.dtype)
            _, o = jax.lax.scan(step, S0, (toN(A), toN(v_scaled), toN(wk_scaled_dec), toN(rk_decay), toN(intra), toN(wk_pos), jnp.moveaxis(chunk_end_decay, 2, 0)))
            o = jnp.moveaxis(o, 0, 2).reshape(Bs, H, Tp, d)
            o = jnp.swapaxes(o, 1, 2).reshape(Bs, Tp, Ds)[:, :Ts]
            return out + jnp.einsum('btd,ed->bte', o, W_read).astype(out.dtype)
        return _forward(out, W_write, W_read, W_alpha, W_beta, A_log, dt_bias)

    def _L0_ffn_ref(x, router_w, router_b, expert_up, expert_down):
        import jax, jax.numpy as jnp
        import numpy as np
        D_MODEL = 128
        N_EXPERTS = 8
        TOP_K = 2
        B, S, D = x.shape
        E = expert_up.shape[0]
        x_flat = x.reshape(-1, D)
        logits = x_flat @ router_w + router_b
        probs = jax.nn.softmax(logits, axis=-1)
        top_w, top_idx = jax.lax.top_k(probs, TOP_K)
        comb = jnp.sum(top_w[..., None] * jax.nn.one_hot(top_idx, E, dtype=x.dtype), axis=1)
        output = jnp.zeros_like(x_flat)
        for e in range(E):
            h = jax.nn.gelu(x_flat @ expert_up[e].T, approximate=False)
            out_e = h @ expert_down[e].T
            output = output + comb[:, e:e + 1] * out_e
        return output.reshape(B, S, D)

    def _L1_xattn_ref(x, latents, Wq, Wkv, Wout, gm, bm, gl, bl):
        import jax, jax.numpy as jnp
        import numpy as np
        D_MODEL = 128
        D_HEAD = 64
        NHEADS = 8
        IN_DIM = D_HEAD * NHEADS
        EPS = 1e-05

        def layernorm(x, g, b):
            mu = jnp.mean(x, axis=-1, keepdims=True)
            var = jnp.var(x, axis=-1, keepdims=True)
            return (x - mu) * jax.lax.rsqrt(var + EPS) * g + b
        scale = D_HEAD ** (-0.5)
        xn = layernorm(x, gm, bm)
        ln = layernorm(latents, gl, bl)
        q = ln @ Wq
        kv_input = jnp.concatenate([xn, ln], axis=-2)
        kv = kv_input @ Wkv
        k, v = jnp.split(kv, 2, axis=-1)

        def heads(t):
            B, S, _ = t.shape
            return t.reshape(B, S, NHEADS, D_HEAD).transpose(0, 2, 1, 3)
        q, k, v = (heads(q), heads(k), heads(v))
        q = q / scale
        sim = jnp.einsum('bhid,bhjd->bhij', q, k)
        sim = sim - jax.lax.stop_gradient(jnp.max(sim, axis=-1, keepdims=True))
        attn = jax.nn.softmax(sim, axis=-1)
        out = jnp.einsum('bhij,bhjd->bhid', attn, v)
        B, H, L, dh = out.shape
        out = out.transpose(0, 2, 1, 3).reshape(B, L, H * dh)
        return out @ Wout

    def _L1_attn_ref(x, W_in, conv_x_w, conv_x_b, conv_z_w, conv_z_b, W_q, W_k, W_v, W_g, W_gk, W_b, b_b, A_log, dt_bias, g_norm_w, W_so, W_out):
        import jax, jax.numpy as jnp
        import numpy as np
        import math
        B, L, D_MODEL = (8, 256, 128)
        D_INNER, D_SSM = (256, 128)
        KEY_DIM, VALUE_DIM, H = (96, 192, 4)
        DK, DV = (KEY_DIM // H, VALUE_DIM // H)
        D_CONV = 4
        EPS = 1e-05

        def _dwconv(x, w, b):
            y = jax.lax.conv_general_dilated(x, w, window_strides=(1,), padding=[(1, 2)], dimension_numbers=('NCH', 'OIH', 'NCH'), feature_group_count=x.shape[1])
            return y + b[None, :, None]

        def _l2norm(x):
            return x * jax.lax.rsqrt(jnp.sum(x * x, axis=-1, keepdims=True) + 1e-06)

        def _gated_delta_rule(q, k, v, beta, gk):
            qT = jnp.moveaxis(q, 2, 0)
            kT = jnp.moveaxis(k, 2, 0)
            vT = jnp.moveaxis(v, 2, 0)
            bT = jnp.moveaxis(beta, 2, 0)
            gT = jnp.moveaxis(gk, 2, 0)
            S0 = jnp.zeros((q.shape[0], q.shape[1], q.shape[3], v.shape[3]), q.dtype)

            def step(S, inp):
                qt, kt, vt, bt, gt = inp
                S = S * jnp.exp(gt)[..., None, None]
                u = bt[..., None] * (vt - jnp.einsum('bhk,bhkv->bhv', kt, S))
                S = S + jnp.einsum('bhk,bhv->bhkv', kt, u)
                ot = jnp.einsum('bhk,bhkv->bhv', qt, S)
                return (S, ot)
            _, o = jax.lax.scan(step, S0, (qT, kT, vT, bT, gT))
            return jnp.moveaxis(o, 0, 2)
        b, l, _ = x.shape
        xz = jnp.swapaxes(x @ W_in, 1, 2)
        xc, zc = jnp.split(xz, 2, axis=1)
        xs = jax.nn.silu(_dwconv(xc, conv_x_w, conv_x_b))
        zs = jax.nn.silu(_dwconv(zc, conv_z_w, conv_z_b))
        xs = jnp.swapaxes(xs, 1, 2)
        q = (xs @ W_q).reshape(b, l, H, DK).transpose(0, 2, 1, 3)
        k = (xs @ W_k).reshape(b, l, H, DK).transpose(0, 2, 1, 3)
        v = (xs @ W_v).reshape(b, l, H, DV).transpose(0, 2, 1, 3)
        gk = -jnp.exp(A_log) * jax.nn.softplus(xs @ W_gk + dt_bias)
        gk = jnp.swapaxes(gk, 1, 2)
        beta = jnp.swapaxes(jax.nn.sigmoid(xs @ W_b + b_b), 1, 2)
        q = _l2norm(q)
        k = _l2norm(k)
        o = _gated_delta_rule(q, k, v, beta, gk)
        o = o.transpose(0, 2, 1, 3)
        g = (xs @ W_g).reshape(b, l, H, DV)
        o = o * jax.lax.rsqrt(jnp.mean(o * o, axis=-1, keepdims=True) + EPS) * g_norm_w
        o = o * (g * jax.nn.sigmoid(g))
        o = o.reshape(b, l, VALUE_DIM)
        y = o @ W_so
        y = jnp.concatenate([y, jnp.swapaxes(zs, 1, 2)], axis=-1)
        return y @ W_out

    def _L1_ffn_ref(hidden_states, ln1_weight, ln1_bias, ln2_weight, ln2_bias, qkv_weight, proj_weight, router_weight, moe_w1, moe_w2):
        import jax, jax.numpy as jnp
        import numpy as np
        EPS = 1e-05
        NUM_HEADS = 16
        NUM_KV_HEADS = 4
        NUM_EXPERTS = 8
        TOP_K = 2

        def _layernorm(x, w, b):
            mu = jnp.mean(x, axis=-1, keepdims=True)
            var = jnp.mean((x - mu) ** 2, axis=-1, keepdims=True)
            return (x - mu) * jax.lax.rsqrt(var + EPS) * w + b
        S, B, H = hidden_states.shape
        hd = H // NUM_HEADS
        rep = NUM_HEADS // NUM_KV_HEADS
        scale = 1.0 / hd ** 0.5
        ln1_out = _layernorm(hidden_states, ln1_weight, ln1_bias)
        qkv = jnp.einsum('sbh,oh->sbo', ln1_out, qkv_weight)
        q = qkv[..., :NUM_HEADS * hd].reshape(S, B, NUM_HEADS, hd)
        k = qkv[..., NUM_HEADS * hd:(NUM_HEADS + NUM_KV_HEADS) * hd].reshape(S, B, NUM_KV_HEADS, hd)
        v = qkv[..., (NUM_HEADS + NUM_KV_HEADS) * hd:].reshape(S, B, NUM_KV_HEADS, hd)
        k = jnp.repeat(k, rep, axis=2)
        v = jnp.repeat(v, rep, axis=2)
        scores = jnp.einsum('sbhd,tbhd->bhst', q, k) * scale
        causal = jnp.tril(jnp.ones((S, S), bool))
        scores = jnp.where(causal, scores, jnp.finfo(scores.dtype).min)
        probs = jax.nn.softmax(scores, axis=-1)
        attn = jnp.einsum('bhst,tbhd->sbhd', probs, v).reshape(S, B, H)
        proj_out = jnp.einsum('sbh,oh->sbo', attn, proj_weight)
        hidden_after_attn = hidden_states + proj_out
        ln2_out = _layernorm(hidden_after_attn, ln2_weight, ln2_bias)
        x = ln2_out.reshape(-1, H)
        logits = jnp.einsum('th,eh->te', x, router_weight)
        gate = jax.nn.softmax(logits, axis=-1)
        top_probs, top_idx = jax.lax.top_k(gate, TOP_K)
        h_mid = jax.nn.gelu(jnp.einsum('th,ehf->etf', x, moe_w1))
        expert_out = jnp.einsum('etf,efh->eth', h_mid, moe_w2)
        e_ids = jnp.arange(NUM_EXPERTS)[:, None, None]
        weights = jnp.sum(jnp.where(top_idx[None] == e_ids, top_probs[None], 0.0), axis=-1)
        moe_out = jnp.einsum('eth,et->th', expert_out, weights).reshape(S, B, H)
        return hidden_after_attn + moe_out
    x = x + _L0_xattn_ref(_layernorm(x, axis=-1), ctx_1024, ctx_1024, mask_BxS2_ik0, L0_xattn_Wq, L0_xattn_bq, L0_xattn_Wk, L0_xattn_bk, L0_xattn_Wv, L0_xattn_bv, L0_xattn_Wo, L0_xattn_bo)
    x = x + _L0_attn_ref(_layernorm(x, axis=-1), L0_attn_W_write, L0_attn_W_read, L0_attn_W_alpha, L0_attn_W_beta, L0_attn_A_log, L0_attn_dt_bias)
    x = x + _L0_ffn_ref(_layernorm(x, axis=-1), L0_ffn_router_w, L0_ffn_router_b, L0_ffn_expert_up, L0_ffn_expert_down)
    x = x + _L1_xattn_ref(ctx_1024, _layernorm(x, axis=-1), L1_xattn_Wq, L1_xattn_Wkv, L1_xattn_Wout, L1_xattn_gm, L1_xattn_bm, L1_xattn_gl, L1_xattn_bl)
    x = x + _L1_attn_ref(_layernorm(x, axis=-1), L1_attn_W_in, L1_attn_conv_x_w, L1_attn_conv_x_b, L1_attn_conv_z_w, L1_attn_conv_z_b, L1_attn_W_q, L1_attn_W_k, L1_attn_W_v, L1_attn_W_g, L1_attn_W_gk, L1_attn_W_b, L1_attn_b_b, L1_attn_A_log, L1_attn_dt_bias, L1_attn_g_norm_w, L1_attn_W_so, L1_attn_W_out)
    x = x + _L1_ffn_ref(_layernorm(x, axis=-1), L1_ffn_ln1_weight, L1_ffn_ln1_bias, L1_ffn_ln2_weight, L1_ffn_ln2_bias, L1_ffn_qkv_weight, L1_ffn_proj_weight, L1_ffn_router_weight, L1_ffn_moe_w1, L1_ffn_moe_w2)
    return x

_drawn_inputs = setup_inputs


def setup_inputs(seed=0):
    import zlib

    import numpy as np

    out = dict(_drawn_inputs(seed))
    spreads = {'L0_xattn_bq': (0.0, 0.1),
     'L0_xattn_bk': (0.0, 2.0),
     'L0_xattn_bv': (0.0, 0.1),
     'L0_xattn_bo': (0.0, 0.1),
     'L0_ffn_router_b': (0.0, 0.1),
     'L1_xattn_gm': (1.0, 0.2),
     'L1_xattn_bm': (0.0, 0.1),
     'L1_xattn_gl': (1.0, 0.2),
     'L1_xattn_bl': (0.0, 0.1),
     'L1_attn_conv_x_b': (0.0, 0.357),
     'L1_attn_conv_z_b': (0.0, 0.407),
     'L1_attn_b_b': (0.0, 2.0),
     'L1_attn_g_norm_w': (1.0, 0.6),
     'L1_ffn_ln1_weight': (1.0, 0.6),
     'L1_ffn_ln1_bias': (0.0, 0.8),
     'L1_ffn_ln2_weight': (1.0, 0.6),
     'L1_ffn_ln2_bias': (0.0, 0.8)}
    factors = {'L0_attn_W_write': 8.0,
     'L0_attn_W_read': 8.0,
     'L0_attn_W_alpha': 8.0,
     'L0_attn_W_beta': 8.0,
     'L1_attn_W_gk': 4.606,
     'L1_attn_A_log': 16.301,
     'L1_ffn_qkv_weight': 8.0,
     'L1_ffn_proj_weight': 8.0,
     'L1_ffn_router_weight': 8.0,
     'L1_ffn_moe_w1': 8.0,
     'L1_ffn_moe_w2': 8.0,
     'L1_attn_W_b': 5.82,
     'L1_attn_dt_bias': 3.376}
    for name, (base, spread) in spreads.items():
        noise = np.random.default_rng([zlib.crc32(name.encode()), seed]).standard_normal(out[name].shape)
        drawn = base * np.exp(spread * noise) if base else spread * noise
        out[name] = jnp.asarray(drawn.astype(out[name].dtype))
    for name, factor in factors.items():
        out[name] = (out[name] * factor).astype(out[name].dtype)
    return out
```

```python
from contextlib import ExitStack

import concourse.bass as bass
from concourse import mybir

ALU = mybir.AluOpType
ACT = mybir.ActivationFunctionType
AXX = mybir.AxisListType.X
F32 = mybir.dt.float32
BF16 = mybir.dt.bfloat16
I32 = mybir.dt.int32
U32 = mybir.dt.uint32

P = 128
D = 128
B = 32
T = 64
NT = B * T // P
S = 1601
KF = S // P
SR = S - KF * P
NK = KF + 1
LN_EPS = 1e-5
LEVELS = 6
MASKED = -1e30
CREDIT = 4


def wait(eng, sem, count):
    if isinstance(count, int) and count <= 0:
        return
    eng.wait_ge(sem, count + CREDIT)


def wcols(k):
    return P if k < KF else SR


def ccols(c):
    return 512 * c, min(512, S - 512 * c)


class Kernel:

    def __init__(self, nc, ctx, dram):
        self.nc, self.ctx, self.dram = nc, ctx, dram
        self.credited = []

    def sb(self, name, shape, dt=F32, ctx=None):
        return (ctx or self.ctx).enter_context(self.nc.sbuf_tensor("sb_" + name, shape, dt))

    def ps(self, name, shape, dt=F32, ctx=None):
        return (ctx or self.ctx).enter_context(self.nc.psum_tensor("ps_" + name, shape, dt))

    def sem(self, name):
        s = self.nc.alloc_semaphore(name=name)
        self.stage.append(s)
        return s

    def counted(self, name):
        s = self.sem(name)
        self.credited.append(s)
        return s

    def run(self, sems, body):
        self.stage, self.credited = [], []
        s = sems(self)
        credited = self.credited
        with self.nc.Block() as block:
            @block.gpsimd
            def _(pool):
                for c in credited:
                    pool.sem_inc(c, CREDIT)
        body(self, s)
        self.nc.clear_and_free_semaphores(self.stage)


def setup_sems(k):
    return {n: k.sem(n) for n in ("made", "cmade", "ld_x", "ld_w0", "ld_m", "bias", "st_m")}


def stage_setup(k, s):
    nc, d = k.nc, k.dram
    k.x = k.sb("x", [P, NT, D])
    k.hn = k.sb("hn", [P, NT, D])
    k.hT = k.sb("hT", [P, NT * P])
    k.st6 = k.sb("st6", [P, NT, 6])
    k.mv = k.sb("mv", [P, NT, 2])
    k.rstd = k.sb("rstd", [P, NT])
    k.cmv = k.sb("cmv", [P, B, NK, 2])
    k.crstd = k.sb("crstd", [P, B, NK])
    k.ident = k.sb("ident", [P, P])
    k.ones = k.sb("ones", [P, P])
    k.onesb = k.sb("onesb", [P, P], BF16)
    k.half = k.sb("half", [P, 32])
    k.heads = k.sb("heads", [P, 16])
    k.subhead = k.sb("subhead", [P, 4])
    k.negdiag = k.sb("negdiag", [P, 8, P], BF16)
    k.U, k.SU, k.SL = (k.sb(n, [P, P]) for n in ("U", "SU", "SL"))
    k.LV = [k.sb(f"LV{l}", [P, P]) for l in range(LEVELS)]
    k.quad = k.sb("quad", [P, 4])
    k.rank = k.sb("rank", [P, 8])
    made, cmade, ld_x, ld_w0 = (s[n] for n in ("made", "cmade", "ld_x", "ld_w0"))
    k.w0 = {n: k.sb(f"w0{n}", [P, P]) for n in "qkvo"}
    k.w0Ta = k.sb("w0T", [P, 4 * P])
    k.w0T = {n: k.w0Ta[:, P * i:P * i + P] for i, n in enumerate("qkvo")}
    k.bq = k.sb("bq", [P, 1])
    k.bk = k.sb("bk", [P, 1])
    k.bvB = k.sb("bvB", [P, P])
    k.boB = k.sb("boB", [P, P])
    ctx = ExitStack()
    maskI = k.sb("su_maskI", [B, S], I32, ctx)
    maskF = k.sb("su_maskF", [B, S], F32, ctx)
    k.bias_rows = d["out"].rearrange("b t d -> (b t d)")[0:B * S].rearrange("(b s) -> b s", s=S)
    with nc.Block() as block:
        @block.sync
        def _(sp):
            sp.dma_start(maskI[:, :], d["mask_BxS2_ik0"]).then_inc(s["ld_m"], 16)
            sp.dma_start(k.x[:, :, :], d["x"].rearrange("b t d -> (b t) d").rearrange("(n p) d -> p n d", p=P)).then_inc(ld_x, 16)
            for n in "qkvo":
                sp.dma_start(k.w0[n][:, :], d[f"L0_xattn_W{n}"]).then_inc(ld_w0, 16)
            for t, n in ((k.bq, "q"), (k.bk, "k")):
                sp.dma_start(t[:, :], d[f"L0_xattn_b{n}"].rearrange("(d a) -> d a", a=1)).then_inc(ld_w0, 16)
            for t, n in ((k.bvB, "v"), (k.boB, "o")):
                sp.dma_start(t[:, :], d[f"L0_xattn_b{n}"].partition_broadcast(P)).then_inc(ld_w0, 16)
            sp.wait_ge(ld_w0, 16 * 8)
            sp.wait_ge(ld_x, 16)
            sp.wait_ge(s["bias"], 1)
            sp.dma_start(k.bias_rows, maskF[:, :]).then_inc(s["st_m"], 16)
            sp.wait_ge(s["st_m"], 16)

        @block.vector
        def _(v):
            v.wait_ge(s["ld_m"], 16)
            v.tensor_scalar(maskF[:, :], maskI[:, :], 0.0, MASKED, ALU.is_equal, ALU.mult).then_inc(s["bias"], 1)

        @block.gpsimd
        def _(pool):
            for t, v in ((k.ident, 0.0), (k.ones, 1.0), (k.onesb, 1.0), (k.half, -0.5), (k.heads, 1.0), (k.subhead, 1.0)):
                pool.memset(t[:, :], v).then_inc(made, 1)
            pool.memset(k.negdiag[:, :, :], 0.0).then_inc(made, 1)
            pool.wait_ge(made, 7)
            pool.affine_select(out=k.ident[:, :], in_=k.ident[:, :], compare_op=ALU.not_equal, fill=1.0, base=0,
                               pattern=[[-1, P]], channel_multiplier=1).then_inc(made, 1)
            pool.affine_select(out=k.negdiag[:, :, :], in_=k.negdiag[:, :, :], compare_op=ALU.not_equal, fill=-1.0,
                               base=-96, pattern=[[-1, 8], [0, P]], channel_multiplier=1).then_inc(made, 1)
            pool.affine_select(out=k.heads[:, :], in_=k.heads[:, :], compare_op=ALU.is_ge, fill=0.0, base=0,
                               pattern=[[-8, 16]], channel_multiplier=1).then_inc(made, 1)
            pool.wait_ge(made, 10)
            pool.affine_select(out=k.heads[:, :], in_=k.heads[:, :], compare_op=ALU.is_ge, fill=0.0, base=7,
                               pattern=[[8, 16]], channel_multiplier=-1).then_inc(made, 1)
            pool.wait_ge(made, 11)
            pool.tensor_tensor(k.subhead[:, :], k.heads[:, 0:4], k.heads[:, 4:8], ALU.add).then_inc(made, 1)
            for g in (2, 3):
                pool.wait_ge(made, 10 + g)
                pool.tensor_tensor(k.subhead[:, :], k.subhead[:, :], k.heads[:, 4 * g:4 * g + 4], ALU.add).then_inc(made, 1)
            pool.iota(k.rank[:, :], pattern=[[-1, 8]], base=8, channel_multiplier=0,
                      allow_small_or_imprecise_dtypes=True).then_inc(made, 1)
            pool.memset(k.quad[:, :], 0.0).then_inc(made, 1)
            for g in range(4):
                pool.wait_ge(made, 16 + g)
                pool.memset(k.quad[32 * g:32 * g + 32, g:g + 1], 1.0).then_inc(made, 1)
            pool.wait_ge(made, 20)
            pool.affine_select(out=k.negdiag[:, :, :], in_=k.negdiag[:, :, :], compare_op=ALU.not_equal, fill=-1.0,
                               base=0, pattern=[[-1, 8], [0, P]], channel_multiplier=1).then_inc(made, 1)
            pool.wait_ge(made, 21)
            core_consts(k, pool, cmade)
    ctx.close()


def norm_sems(k, tag):
    return {n: k.sem(f"{tag}_{n}") for n in ("stats", "mean", "rstd", "plain", "norm", "turned", "copied")}


def norm_vector(k, v, s, src=None, dst=None, gain=None, shift=None):
    src, dst = src or k.x, dst or k.hn
    for n in range(NT):
        v.bn_stats(k.st6[:, n, :], src[:, n, :]).then_inc(s["stats"], 1)
    for n in range(NT):
        v.wait_ge(s["stats"], n + 1)
        v.bn_aggr(k.mv[:, n, :], k.st6[:, n, :]).then_inc(s["mean"], 1)
    v.wait_ge(s["mean"], NT)
    v.tensor_scalar(k.rstd[:, :], k.mv[:, :, 1], LN_EPS, None, ALU.add).then_inc(s["mean"], 1)
    v.wait_ge(s["rstd"], 1)
    done = "norm" if gain is None else "plain"
    for n in range(NT):
        v.tensor_scalar(dst[:, n, :], src[:, n, :], k.mv[:, n, 0:1], k.rstd[:, n:n + 1], ALU.subtract, ALU.mult)\
         .then_inc(s[done], 1)
    if gain is not None:
        v.wait_ge(s["plain"], NT)
        v.tensor_tensor(dst[:, :, :], dst[:, :, :], gain[:, :].unsqueeze(1).to_broadcast([P, NT, D]), ALU.mult).then_inc(s["plain"], 1)
        v.wait_ge(s["plain"], NT + 1)
        v.tensor_tensor(dst[:, :, :], dst[:, :, :], shift[:, :].unsqueeze(1).to_broadcast([P, NT, D]), ALU.add).then_inc(s["norm"], NT)


def norm_pool(k, pool, s):
    pool.wait_ge(s["mean"], NT + 1)
    pool.tensor_tensor(k.rstd[:, :], k.rstd[:, :], k.half[:, 0:NT], ALU.pow).then_inc(s["rstd"], 1)


def norm_tensor(k, pe, s, banks, src=None):
    src = src or k.hn
    for c in range(NT // 4):
        if c >= 2:
            pe.wait_ge(s["copied"], c - 1)
        for j in range(4):
            n = 4 * c + j
            pe.wait_ge(s["norm"], n + 1)
            mm = pe.transpose(banks[c % 2][:, P * j:P * j + P], src[:, n, :], k.ident[:, :])
        mm.then_inc(s["turned"], 1)


def norm_scalar(k, act, s, banks):
    for c in range(NT // 4):
        act.wait_ge(s["turned"], c + 1)
        act.activation(k.hT[:, 512 * c:512 * c + 512], banks[c % 2][:, :], ACT.Copy).then_inc(s["copied"], 1)


def stage_xattn0(k, s):
    nc, d = k.nc, k.dram
    H, DH, G = 16, 8, 4
    SCALE = DH ** -0.5
    HQ = H * T
    NP = HQ // P
    ctx = ExitStack()
    sb = lambda n, s, dt=F32: k.sb("a0_" + n, s, dt, ctx)
    C = [sb(f"C{i}", [P, KF, D]) for i in range(2)]
    CR = [sb(f"CR{i}", [SR, D]) for i in range(2)]
    CT = sb("CT", [P, S])
    K1, K2, K3 = (sb(n, [P, S], BF16) for n in ("K1", "K2", "K3"))
    RK = sb("RK", [P, S])
    KS = [[sb(f"KS{i}{w}", [P, 4, S], BF16) for w in range(2)] for i in range(2)]
    QS = [[sb(f"QS{i}{w}", [P, 4, G * T], BF16) for w in range(2)] for i in range(2)]
    Sel = sb("Sel", [P, 3, 4, P], BF16)
    V = [sb(f"V{i}", [P, NK, D]) for i in range(2)]
    Qxb = sb("Qxb", [P, H, T], BF16)
    PT = [sb(f"PT{i}", [P, HQ]) for i in range(3)]
    acc = [sb(f"acc{i}", [P, HQ]) for i in range(2)]
    QT = k.hn[:, :, :].rearrange("p n d -> p (n d)")
    OT = k.hT
    Q1, Q2, Q3 = (sb(n, [P, B * T], BF16) for n in ("Q1", "Q2", "Q3"))
    maskI = sb("maskI", [P, B, NK], I32)
    maskP = sb("maskP", [P, B, NK])
    rowF = sb("rowF", [P, S])
    bqs = sb("bqs", [P, 1])
    NU = 26
    NPREP = 13
    cst = sb("cst", [P, NK, 6])
    cag = sb("cag", [P, NK, 2])
    ceps = [sb(f"ceps{i}", [P, NK]) for i in range(2)]
    mx = sb("mx", [P, NP, 4])
    mr = sb("mr", [P, NP, SR])
    mxm = sb("mxm", [P, P])
    junk = sb("junk", [P, 2, 512], BF16)
    rs = sb("rs", [P, G * T])
    pvs = sb("pvs", [P, 2, G * T])
    on = sb("on", [P, G, T])
    SC = [k.ps(f"a0_SC{i}", [P, HQ], F32, ctx) for i in range(2)]
    PV = k.ps("a0_PV", [P, 2, G * T], F32, ctx)
    A = [k.ps(f"a0_A{i}", [P, 512], F32, ctx) for i in range(2)]
    M = k.ps("a0_M", [P, 512], F32, ctx)

    def bank(u):
        return (A[0], A[1], M)[u % 3]

    FIRST = 5

    def units(j):
        return range(2 * j + 2, min(2 * j + 4, NPREP))

    def top_units(j):
        n = NK - FIRST
        return range(NU * (j - FIRST) // n, NU * (j - FIRST + 1) // n) if j >= FIRST else range(0)

    def freed(eng, b, u):
        if u < 4:
            wait(eng, s["ct"], 4 * b + u + 1)
        elif u < 8:
            wait(eng, s["kt"], 4 * b + u - 3)
        elif u < 12:
            wait(eng, s["v"], 4 * b + u - 7)

    def stacked(eng, b, a, before=False):
        if before:
            if not (isinstance(b, int) and b == 0):
                eng.wait_ge(s[f"ldk{1 - a}"], 192 * (b + a))
        else:
            eng.wait_ge(s[f"ldk{a}"], 192 * (b - a) + 384)

    def dsl(b):
        return bass.ds(b, 1)

    def slot(a, j):
        return (a + j) % 3

    def last_use(a, j):
        order = [slot(1 - a, y) for y in range(NK)] + [slot(a, y) for y in range(j)]
        return next(n for n in range(1, len(order) + 1) if order[-n] == slot(a, j))

    def added(b, a, j):
        past = j - last_use(a, j)
        if past < 0:
            return (NK - 1) * (b - 1) + past + NK
        return (NK - 1) * b + max(past, 1)

    PVf = PV[:, :, :].rearrange("p a n -> p (a n)")
    with nc.Block() as block:
        @block.sync
        def _(sp):
            sp.dma_start(maskI[:, :, 0:KF], d["mask_BxS2_ik0"][:, 0:KF * P].rearrange("b (p j) -> p b j", p=P)).then_inc(s["ldm"], 16)
            sp.dma_start(maskI[0:SR, :, KF:NK], d["mask_BxS2_ik0"][:, KF * P:S].rearrange("b (p j) -> p b j", j=1),
                         allow_slow_non_contiguous=True).then_inc(s["ldm"], 16)

            def load(b, a):
                wait(sp, s["ct"], 4 * (b - 1))
                wait(sp, s["cs"], NK * (b - 1))
                sp.dma_start(C[a][:, :, :], d["ctx_1024"][dsl(b), 0:KF * P, :].rearrange("o (p j) d -> p (o j) d", p=P))\
                  .then_inc(s[f"ld{a}"], 16)
                sp.dma_start(CR[a][:, :], d["ctx_1024"][dsl(b), KF * P:S, :].rearrange("o p d -> p (o d)"))\
                  .then_inc(s[f"ld{a}"], 16)

            def row(b):
                wait(sp, s["mx"], b)
                sp.dma_start(rowF[:, :], k.bias_rows[dsl(b), :].rearrange("o s -> (o s)").partition_broadcast(P))\
                  .then_inc(s["ldr"], 16)

            def stack(b, a):
                wait(sp, s["pv"], NK * (b - 1))
                for part, ready, places in ((K1, "k1", ((0, 0), (1, 0), (1, 2))), (K2, "k2", ((0, 1), (1, 1))), (K3, "k3", ((0, 2),))):
                    wait(sp, s[ready], 4 * b + 4)
                    for w, r in places:
                        for g in range(4):
                            sp.dma_start(KS[a][w][32 * r:32 * r + 32, g, :], part[32 * g:32 * g + 32, :]).then_inc(s[f"ldk{a}"], 16)

            load(0, 0)
            row(0)
            load(1, 1)
            sp.wait_ge(s["pz"], 7)
            stack(0, 0)
            row(1)
            stack(1, 1)
            with sp.Fori(0, B // 2 - 1) as i:
                load(2 * i + 2, 0)
                row(2 * i + 2)
                stack(2 * i + 2, 0)
                load(2 * i + 3, 1)
                row(2 * i + 3)
                stack(2 * i + 3, 1)

        @block.gpsimd
        def _(pool):
            norm_pool(k, pool, s["n"])
            pool.wait_ge(s["n"]["rstd"], 1)
            pz = 0
            for t, x in [(KS[i][0], 1.0) for i in range(2)] + [(KS[i][1], 0.0) for i in range(2)] + [(QS[i][1], 0.0) for i in range(2)]:
                pool.memset(t[96:P, :, :], x).then_inc(s["pz"], 1)
                pz += 1
                pool.wait_ge(s["pz"], pz)
            pool.memset(mxm[:, :], 0.0).then_inc(s["pz"], 1)
            pool.wait_ge(s["pz"], 7)
            pool.wait_ge(s["q3"], 1)

            def spread_q(b):
                wait(pool, s["mx"], b)
                pool.tensor_tensor(Qxb[:, :, :], Q1[:, bass.ds(b * T, T)].unsqueeze(1).to_broadcast([P, H, T]),
                                   k.heads[:, :].unsqueeze(2).to_broadcast([P, H, T]), ALU.mult).then_inc(s["qb"], 1)

            def sums(b, a):
                for j in range(1, NK):
                    g = NK * b + j
                    n = wcols(j)
                    wait(pool, s["exp"], g + 1)
                    if j == 1:
                        wait(pool, s["sum"], b - 1)
                        first = PT[slot(a, 0)]
                    else:
                        wait(pool, s["acc"], (NK - 1) * b + j - 1)
                        first = acc[a]
                    pool.tensor_tensor(acc[a][0:n, :], first[0:n, :], PT[slot(a, j)][0:n, :], ALU.add)\
                        .then_inc(s["acc"], 1)

            def spread(b, a):
                wait(pool, s["ce"], b + 1)
                pool.tensor_tensor(k.crstd[:, bass.ds(b, 1), :].rearrange("p o j -> p (o j)"), ceps[a][:, :], k.half[:, 0:NK], ALU.pow)\
                    .then_inc(s["cp"], 1)

            spread_q(0)
            spread_q(1)
            spread(0, 0)
            sums(0, 0)
            with pool.Fori(0, B // 2 - 1) as i:
                for a, b in ((1, 2 * i + 1), (0, 2 * i + 2)):
                    spread_q(b + 1)
                    spread(b, a)
                    sums(b, a)
            spread(B - 1, 1)
            sums(B - 1, 1)

        @block.scalar
        def _(act):
            act.wait_ge(s["w"], 1)
            act.activation(k.w0Ta[:, :], PVf, ACT.Copy).then_inc(s["wc"], 1)
            norm_scalar(k, act, s["n"], A)
            act.wait_ge(s["wc"], 2)
            for c in range(NT // 4):
                act.wait_ge(s["q"], c + 1)
                act.activation(QT[:, 512 * c:512 * c + 512], M[:, :], ACT.Identity,
                               bias=bqs[:, :], scale=SCALE).then_inc(s["qc"], 1)

            def turned(b, a, c):
                c0, n = ccols(c)
                wait(act, s["tt"], 4 * b + c + 1)
                if c == 0:
                    wait(act, s["vp"], 4 * b)
                act.activation(CT[:, c0:c0 + n], bank(c)[:, 0:n], ACT.Copy).then_inc(s["ct"], 1)

            def keys(b, a, c):
                c0, n = ccols(c)
                wait(act, s["kp"], 4 * b + c + 1)
                if c == 0:
                    stacked(act, b, a, before=True)
                    wait(act, s["mx"], b)
                act.activation(K1[:, c0:c0 + n], bank(4 + c)[:, 0:n], ACT.Identity, bias=k.bk[:, :]).then_inc(s["k1"], 1)

            def second(b, c):
                c0, n = ccols(c)
                wait(act, s["kt"], 4 * b + c + 1)
                act.activation(K2[:, c0:c0 + n], RK[:, c0:c0 + n], ACT.Copy).then_inc(s["k2"], 1)

            def queries(b, a):
                wait(act, s["ql"], b + 1)
                wait(act, s["pv"], NK * (b - 1))
                for w in range(2):
                    for h in range(G):
                        act.activation(QS[a][w][0:96, :, T * h:T * h + T],
                                       bank(12)[0:96, 4 * T * w:4 * T * w + 4 * T].rearrange("p (g q) -> p g q", q=T),
                                       ACT.Copy, scale=k.subhead[0:96, h:h + 1]).then_inc(s["qa"], 1)

            def prep(b, a, u):
                if u < 4:
                    turned(b, a, u)
                elif u < 8:
                    keys(b, a, u - 4)
                if 5 <= u < 9:
                    second(b, u - 5)
                if u == 12:
                    queries(b, a)

            def probs(b, a, j):
                g = NK * b + j
                n = wcols(j)
                wait(act, s["sc"], g + 1)
                old = g - last_use(a, j) + 1
                wait(act, s["pv"], old)
                wait(act, s["acc"], added(b, a, j))
                act.activation(PT[slot(a, j)][0:n, :], SC[(a + j) % 2][0:n, :], ACT.Exp,
                               bias=maskP[0:n, dsl(b), j:j + 1].rearrange("p o j -> p (o j)")).then_inc(s["exp"], 1)

            def step(b, a, more):
                if more:
                    prep(b + 1, 1 - a, 0)
                    prep(b + 1, 1 - a, 1)
                for j in range(NK):
                    probs(b, a, j)
                    if more:
                        for u in units(j):
                            prep(b + 1, 1 - a, u)

            act.wait_ge(s["pz"], 7)
            for u in range(NPREP):
                prep(0, 0, u)
            act.wait_ge(s["mp"], 2)
            step(0, 0, True)
            with act.Fori(0, B // 2 - 1) as i:
                step(2 * i + 1, 1, True)
                step(2 * i + 2, 0, True)
            step(B - 1, 1, False)

        @block.vector
        def _(v):
            v.tensor_scalar(bqs[:, :], k.bq[:, :], SCALE, None, ALU.mult).then_inc(s["wc"], 1)
            norm_vector(k, v, s["n"])
            v.wait_ge(s["ldm"], 32)
            v.tensor_scalar(maskP[:, :, 0:KF], maskI[:, :, 0:KF], 0.0, MASKED, ALU.is_equal, ALU.mult).then_inc(s["mp"], 1)
            v.tensor_scalar(maskP[0:SR, :, KF:NK], maskI[0:SR, :, KF:NK], 0.0, MASKED, ALU.is_equal, ALU.mult)\
             .then_inc(s["mp"], 1)
            v.memset(Sel[:, :, :, :], 0.0).then_inc(s["sl"], 1)
            v.wait_ge(s["sl"], 1)
            for w, (lo, n) in enumerate(((0, 3), (0, 2), (2, 1))):
                v.tensor_copy(Sel[:, w, :, 32 * lo:32 * (lo + n)].rearrange("p g (r i) -> p g r i", r=n),
                              k.ident[:, :].rearrange("p (g i) -> p g i", g=4).unsqueeze(2).to_broadcast([P, 4, n, 32])).then_inc(s["sl"], 1)
            v.wait_ge(s["qc"], NT // 4)
            v.tensor_copy(Q1[:, :], QT).then_inc(s["q3"], 1)
            v.wait_ge(s["q3"], 1)
            v.tensor_tensor(QT, QT, Q1[:, :], ALU.subtract).then_inc(s["qr"], 1)
            v.wait_ge(s["qr"], 1)
            v.tensor_copy(Q2[:, :], QT).then_inc(s["qr"], 1)
            v.wait_ge(s["qr"], 2)
            v.tensor_tensor(Q3[:, :], QT, Q2[:, :], ALU.subtract).then_inc(s["qr"], 1)

            def values(b, a, c):
                wait(v, s["vp"], 4 * b + c + 1)
                if c == 0:
                    wait(v, s["pv"], NK * (b - 1))
                n = 4 if c < 3 else 1
                m = P if c < 3 else SR
                v.tensor_tensor(V[a][0:m, 4 * c:4 * c + n, :], bank(8 + c)[0:m, 0:n * D].rearrange("p (j d) -> p j d", d=D),
                                k.bvB[0:m, :].unsqueeze(1).to_broadcast([m, n, D]), ALU.add).then_inc(s["v"], 1)

            def prep(b, a, u):
                if 4 <= u < 8:
                    c0, n = ccols(u - 4)
                    wait(v, s["k1"], 4 * b + u - 3)
                    wait(v, s["k2"], 4 * b)
                    v.scalar_tensor_tensor(out=RK[:, c0:c0 + n], in0=bank(u)[:, 0:n], scalar=k.bk[:, :], in1=K1[:, c0:c0 + n],
                                           op0=ALU.add, op1=ALU.subtract).then_inc(s["kt"], 1)
                if 6 <= u < 10:
                    c0, n = ccols(u - 6)
                    wait(v, s["k2"], 4 * b + u - 5)
                    if u == 6:
                        stacked(v, b, a, before=True)
                    v.tensor_tensor(K3[:, c0:c0 + n], RK[:, c0:c0 + n], K2[:, c0:c0 + n], ALU.subtract).then_inc(s["k3"], 1)
                if 8 <= u < 12:
                    values(b, a, u - 8)

            def stats(b, a):
                v.wait_ge(s[f"ld{a}"], 16 * (b - a) + 32)
                for j in range(NK):
                    m = wcols(j)
                    v.bn_stats(cst[0:m, j, :], C[a][:, j, :] if j < KF else CR[a][:, :]).then_inc(s["cs"], 1)
                for j in range(NK):
                    m = wcols(j)
                    wait(v, s["cs"], NK * b + j + 1)
                    v.sem_inc(s["go_v"], 1)
                    v.bn_aggr(cag[0:m, j, :], cst[0:m, j, :]).then_inc(s["ca"], 1)
                wait(v, s["ca"], NK * (b + 1))
                v.tensor_copy(k.cmv[:, bass.ds(b, 1), :, :].rearrange("p o j e -> p (o j) e"), cag[:, :, :]).then_inc(s["cc"], 1)
                wait(v, s["cp"], b - 1)
                v.tensor_scalar(ceps[a][:, :], cag[:, :, 1], LN_EPS, None, ALU.add).then_inc(s["ce"], 1)

            def tops(b, u):
                wait(v, s["as"], NU * b + u + 1)
                if u == 0:
                    v.wait_ge(s["ldr"], 16 * b + 16)
                if u < 24:
                    p, c = u % NP, u // NP
                    bias = rowF[:, 0:KF * P].rearrange("q (p j) -> q j p", p=P)[:, 4 * c:4 * c + 4, :]
                    wait(v, s["am"], NU * b + u - 1)
                    v.sem_inc(s["go_v"], 1)
                    v.tensor_tensor_reduce(junk[:, u % 2, :].rearrange("q (j p) -> q j p", p=P),
                                           bank(u)[:, :].rearrange("q (j p) -> q j p", p=P), bias,
                                           1.0, MASKED, ALU.add, ALU.max, mx[:, p, c:c + 1]).then_inc(s["am"], 1)
                else:
                    h = 4 * (u - 24)
                    v.tensor_tensor(mr[:, h:h + 4, :], bank(u)[:, 0:4 * SR].rearrange("q (p s) -> q p s", s=SR),
                                    rowF[:, KF * P:S].unsqueeze(1).to_broadcast([P, 4, SR]), ALU.add).then_inc(s["am"], 1)
                    wait(v, s["am"], NU * b + u + 1)
                    v.tensor_reduce(mx[:, h:h + 4, 3], mr[:, h:h + 4, :], AXX, ALU.max).then_inc(s["ar"], 1)

            def top(b, a):
                wait(v, s["ar"], 2 * b + 2)
                v.tensor_reduce(mxm[:, 96:96 + NP], mx[:, :, :], AXX, ALU.max).then_inc(s["m1"], 1)
                wait(v, s["m1"], 2 * b + 1)
                v.tensor_scalar(mxm[:, 96:96 + NP], mxm[:, 96:96 + NP], 0.1 * MASKED, None, ALU.max).then_inc(s["m1"], 1)
                wait(v, s["mt"], b + 1)
                wait(v, s["pv"], NK * (b - 1))
                v.tensor_tensor(QS[a][0][96:P, :, :].rearrange("p g (i c) -> p (g i) c", i=2),
                                M[96:P, 0:P].unsqueeze(1).to_broadcast([32, NP, P]),
                                k.negdiag[96:P, :, :], ALU.mult).then_inc(s["mx"], 1)

            def final(b, a):
                wait(v, s["sum"], b + 1)
                v.tensor_copy(pvs[:, :, :], PV[:, :, :]).then_inc(s["pvc"], 1)
                wait(v, s["pvc"], b + 1)
                v.tensor_scalar(rs[:, :], pvs[:, 1, :], 1e-30, None, ALU.max).then_inc(s["f"], 1)
                wait(v, s["f"], 5 * b + 1)
                v.reciprocal(rs[:, :], rs[:, :]).then_inc(s["f"], 1)
                wait(v, s["f"], 5 * b + 2)
                v.tensor_tensor(rs[:, :].rearrange("p (h q) -> p h q", q=T), rs[:, :].rearrange("p (h q) -> p h q", q=T),
                                k.subhead[:, :].unsqueeze(2).to_broadcast([P, G, T]), ALU.mult).then_inc(s["f"], 1)
                wait(v, s["f"], 5 * b + 3)
                v.tensor_tensor(on[:, :, :].rearrange("p h q -> p (h q)"), pvs[:, 0, :], rs[:, :], ALU.mult).then_inc(s["f"], 1)
                wait(v, s["f"], 5 * b + 4)
                v.tensor_reduce(OT[:, bass.ds(b * T, T)], on[:, :, :].rearrange("p h q -> p q h"), AXX, ALU.add)\
                 .then_inc(s["f"], 1)

            def step(b, a, more):
                if not (isinstance(b, int) and b == 0):
                    final(b - 1, 1 - a)
                if more:
                    for u in range(NPREP):
                        prep(b + 1, 1 - a, u)
                    for u in range(NU):
                        tops(b + 1, u)
                    top(b + 1, 1 - a)
                    stats(b + 1, 1 - a)

            v.memset(cag[:, :, :], 0.0).then_inc(s["cz"], 1)
            v.wait_ge(s["cz"], 1)
            v.wait_ge(s["pz"], 7)
            for u in range(NPREP):
                prep(0, 0, u)
            for u in range(NU):
                tops(0, u)
            top(0, 0)
            stats(0, 0)
            step(0, 0, True)
            with v.Fori(0, B // 2 - 1) as i:
                step(2 * i + 1, 1, True)
                step(2 * i + 2, 0, True)
            step(B - 1, 1, False)
            final(B - 1, 1)
            for n in range(NT):
                v.wait_ge(s["y"], n + 1)
                v.tensor_tensor(k.x[:, n, :], k.x[:, n, :], A[n % 2][:, 0:D], ALU.add).then_inc(s["x"], 1)
                v.wait_ge(s["x"], 2 * n + 1)
                v.tensor_tensor(k.x[:, n, :], k.x[:, n, :], k.boB[:, :], ALU.add).then_inc(s["x"], 1)
            v.wait_ge(s["x"], 2 * NT)

        @block.tensor
        def _(pe):
            for i, n in enumerate("qkvo"):
                mm = pe.transpose(PVf[:, P * i:P * i + P], k.w0[n][:, :], k.ident[:, :])
            mm.then_inc(s["w"], 1)
            norm_tensor(k, pe, s["n"], A)
            pe.wait_ge(s["wc"], 2)
            for c in range(NT // 4):
                pe.wait_ge(s["n"]["copied"], c + 1)
                if c >= 1:
                    pe.wait_ge(s["qc"], c)
                pe.matmul(M[:, :], k.w0T["q"], k.hT[:, 512 * c:512 * c + 512], start=True, stop=True).then_inc(s["q"], 1)
            pe.wait_ge(s["qc"], NT // 4)

            def prep(b, a, u):
                c = u % 4
                c0, n = ccols(c)
                bk = bank(u)
                if u == 0:
                    wait(pe, s["am"], NU * b)
                    pe.wait_ge(s[f"ld{a}"], 16 * (b - a) + 32)
                elif u == 2:
                    wait(pe, s["mx"], b)
                elif u > 2:
                    freed(pe, b, u - 3)
                if u == 4:
                    wait(pe, s["ct"], 4 * b + 4)
                if u < 4:
                    for j in range(4 * c, min(4 * c + 4, NK)):
                        src = C[a][:, j, :] if j < KF else CR[a][:, :]
                        m = wcols(j)
                        mm = pe.transpose(bk[:, P * (j % 4):P * (j % 4) + m], src, k.ident[0:m, 0:m])
                    mm.then_inc(s["tt"], 1)
                elif u < 8:
                    pe.matmul(bk[:, 0:n], k.w0T["k"], CT[:, c0:c0 + n], start=True, stop=True).then_inc(s["kp"], 1)
                elif u < 12:
                    for j in range(4 * c, min(4 * c + 4, NK)):
                        m = wcols(j)
                        mm = pe.matmul(bk[0:m, P * (j % 4):P * (j % 4) + D], CT[:, P * j:P * j + m], k.w0T["v"],
                                       start=True, stop=True)
                    mm.then_inc(s["vp"], 1)
                else:
                    for g in range(4):
                        o = bk[:, T * g:T * g + T]
                        pe.matmul(o, Sel[:, 0, g, :], Q1[:, bass.ds(b * T, T)], start=True, stop=True)
                        o = bk[:, 4 * T + T * g:4 * T + T * g + T]
                        pe.matmul(o, Sel[:, 1, g, :], Q2[:, bass.ds(b * T, T)], start=True, stop=False)
                        mm = pe.matmul(o, Sel[:, 2, g, :], Q3[:, bass.ds(b * T, T)], start=False, stop=True)
                    mm.then_inc(s["ql"], 1)

            def tops(b, u):
                if u == 0:
                    wait(pe, s["qb"], b + 1)
                    wait(pe, s["k1"], 4 * b + 4)
                    wait(pe, s["v"], 4 * b + 4)
                    wait(pe, s["qa"], 2 * G * (b + 1))
                if u >= 3:
                    wait(pe, s["am"], NU * b + u - 2)
                if u < 24:
                    p, c = u % NP, u // NP
                    mm = pe.matmul(bank(u)[:, :], Qxb[:, 2 * p:2 * p + 2, :], K1[:, 512 * c:512 * c + 512], start=True, stop=True)
                else:
                    for i in range(4):
                        p = 4 * (u - 24) + i
                        mm = pe.matmul(bank(u)[:, SR * i:SR * i + SR], Qxb[:, 2 * p:2 * p + 2, :], K1[:, KF * P:S], start=True, stop=True)
                mm.then_inc(s["as"], 1)

            def top(b):
                wait(pe, s["m1"], 2 * b + 2)
                wait(pe, s["am"], NU * (b + 1))
                pe.transpose(M[:, 0:P], mxm[:, :], k.ident[:, :]).then_inc(s["mt"], 1)

            def scores(b, a, j):
                g = NK * b + j
                m = wcols(j)
                if j == 0:
                    wait(pe, s["mx"], b + 1)
                    stacked(pe, b, a)
                wait(pe, s["exp"], g - 1)
                for q in range(4):
                    o = SC[(a + j) % 2][0:m, G * T * q:G * T * q + G * T]
                    for w in range(2):
                        mm = pe.matmul(o, KS[a][w][:, q, P * j:P * j + m], QS[a][w][:, q, :], start=(w == 0), stop=(w == 1))
                mm.then_inc(s["sc"], 1)

            def products(b, a, j):
                m = wcols(j)
                wait(pe, s["exp"], NK * b + j + 1)
                if j == 0:
                    wait(pe, s["pvc"], b)
                for g in range(4):
                    mm = pe.matmul(PV[32 * g:32 * g + 32, 0, :], V[a][0:m, j, 32 * g:32 * g + 32],
                                   PT[slot(a, j)][0:m, G * T * g:G * T * g + G * T], start=(j == 0), stop=(j == NK - 1))
                mm.then_inc(s["pv"], 1)

            def total(b, a):
                wait(pe, s["acc"], (NK - 1) * (b + 1))
                for g in range(4):
                    mm = pe.matmul(PV[32 * g:32 * g + 32, 1, :], k.ones[:, 0:32],
                                   acc[a][:, G * T * g:G * T * g + G * T], start=True, stop=True)
                mm.then_inc(s["sum"], 1)

            def step(b, a, more):
                if more:
                    prep(b + 1, 1 - a, 0)
                    prep(b + 1, 1 - a, 1)
                top(b)
                scores(b, a, 0)
                if not (isinstance(b, int) and b == 0):
                    total(b - 1, 1 - a)
                for j in range(NK):
                    if j + 1 < NK:
                        scores(b, a, j + 1)
                    if more:
                        for u in units(j):
                            prep(b + 1, 1 - a, u)
                    if more:
                        for u in top_units(j)[0:2]:
                            tops(b + 1, u)
                    products(b, a, j)
                    if more:
                        for u in top_units(j)[2:]:
                            tops(b + 1, u)

            pe.wait_ge(s["qr"], 3)
            pe.wait_ge(s["sl"], 4)
            for u in range(NPREP):
                prep(0, 0, u)
            for u in range(NU):
                tops(0, u)
            step(0, 0, True)
            with pe.Fori(0, B // 2 - 1) as i:
                step(2 * i + 1, 1, True)
                step(2 * i + 2, 0, True)
            step(B - 1, 1, False)
            total(B - 1, 1)
            wait(pe, s["f"], 5 * B)
            for n in range(NT):
                if n >= 2:
                    pe.wait_ge(s["x"], 2 * (n - 2) + 1)
                pe.matmul(A[n % 2][:, 0:D], OT[:, P * n:P * n + P], k.w0T["o"], start=True, stop=True).then_inc(s["y"], 1)
    ctx.close()


def xattn0_sems(k):
    s = {n: k.sem("a0_" + n) for n in ("go_v", "cz", "ldm", "ld0", "ld1", "ldr", "ldk0", "ldk1", "q3", "qr", "sl", "w", "wc", "q", "qc", "mp", "pz", "y", "x")}
    s.update({n: k.counted("a0_" + n) for n in ("ct", "tt", "kp", "kt", "vp", "v", "pv", "sc", "exp", "acc", "sum", "k1", "k2", "k3",
                                                 "mx", "qb", "ql", "qa", "as", "am", "ar", "m1", "mt", "f", "pvc",
                                                 "cs", "ca", "cc", "ce", "cp")})
    s["n"] = norm_sems(k, "a0n")
    return s


CORE_SEMS = ("lu", "cum", "lt", "ql", "gl", "gm", "qm", "e", "gq", "em", "emp", "p0", "xx", "x1", "t1", "t1s", "p", "u")


class Core:

    def __init__(self, k, tag, ctx, same_mask):
        self.k = k
        two = lambda n, sh: [k.sb(f"{tag}_{n}{a}", sh, F32, ctx) for a in range(2)]
        self.E = two("E", [P, 4, P])
        self.LT = two("LT", [P, 4, P])
        self.QL = two("QL", [P, 4, P])
        self.Em = [[e, l] for e, l in zip(two("Em", [P, 4, P]), self.LT)]
        self.XX = two("XX", [P, 2, 4, P])
        self.T1s = two("T1s", [P, 4, P])
        self.mask = k.SU if same_mask else k.U
        self.T1 = [k.ps(f"{tag}_T1{a}", [P, 4, P], F32, ctx) for a in range(2)]
        self.W = [k.ps(f"{tag}_W{a}", [P, 4, P], F32, ctx) for a in range(2)]
        self.PP = [k.ps(f"{tag}_PP{a}", [P, 2, 4, P], F32, ctx) for a in range(2)]

    @staticmethod
    def at(i, a, l, n=LEVELS):
        return 2 * (n * i + l) + a + 1

    def decays(self, act, s, i):
        for a in range(2):
            wait(act, s["cum"], 2 * i + a + 1)
            act.activation(self.LT[a][:, :, :], self.T1[a][:, :, :], ACT.Exp).then_inc(s["lt"], 1)

    def copies(self, act, s, i, lo=1, hi=LEVELS):
        for l in range(lo, hi):
            for a in range(2):
                wait(act, s["t1"], self.at(i, a, l - 1, LEVELS - 1))
                act.activation(self.T1s[a][:, :, :], self.T1[a][:, :, :], ACT.Copy).then_inc(s["t1s"], 1)

    def sums(self, pe, s, i):
        for a in range(2):
            wait(pe, s["lu"], 2 * i + a + 1)
            pe.matmul(self.T1[a][:, :, :], self.k.SL[:, :], self.E[a][:, :, :], start=True, stop=True).then_inc(s["cum"], 1)

    def solve(self, pe, s, i, lo=1, hi=LEVELS):
        k = self.k
        for a in range(2 if lo == 1 else 0):
            wait(pe, s["em"], 2 * i + a + 1)
            for u in range(4):
                mm = pe.transpose(self.PP[a][:, 0, u, :], self.Em[a][0][:, u, :], k.ident[:, :])
            mm.then_inc(s["p0"], 1)
        for l in range(lo, hi):
            for a in range(2):
                wait(pe, s["emp"], self.at(i, a, l - 1, LEVELS - 1))
                wait(pe, s["xx"], self.at(i, a, l - 1))
                for u in range(4):
                    mm = pe.matmul(self.T1[a][:, u, :], self.Em[a][l % 2][:, u, :], self.XX[a][:, 0, u, :], start=True, stop=True)
                mm.then_inc(s["t1"], 1)
            for a in range(2):
                wait(pe, s["t1s"], self.at(i, a, l - 1, LEVELS - 1))
                if l == 1:
                    wait(pe, s["qm"], 2 * i + a + 1)
                for u in range(4):
                    if l < LEVELS - 1:
                        pe.matmul(self.PP[a][:, 0, u, :], self.XX[a][:, 1, u, :], self.T1s[a][:, u, :], start=True, stop=True)
                    mm = pe.matmul(self.PP[a][:, 1, u, :], self.T1s[a][:, u, :], self.XX[a][:, 1, u, :], start=True, stop=True)
                mm.then_inc(s["p"], 1)

    def parts(self, pool, s, i):
        for l in range(1, LEVELS):
            for a in range(2):
                g = 2 * i + a
                if l == 1:
                    wait(pool, s["e"], g + 1)
                    wait(pool, s["ql"], g + 1)
                else:
                    wait(pool, s["xx"], self.at(i, a, l - 2))
                    if l == 2:
                        wait(pool, s["x1"], g + 1)
                pool.tensor_tensor(self.Em[a][l % 2][:, :, :], self.E[a][:, :, :],
                                   self.k.LV[l][:, :].unsqueeze(1).to_broadcast([P, 4, P]), ALU.mult).then_inc(s["emp"], 1)

    def spread(self, v, s, i, ld):
        bc = lambda m: m[:, :].unsqueeze(1).to_broadcast([P, 4, P])
        for a in range(2):
            v.tensor_tensor(self.E[a][:, :, :], bc(self.k.U), ld[a].unsqueeze(2).to_broadcast([P, 4, P]), ALU.mult).then_inc(s["lu"], 1)

    def vector(self, v, s, i, beta):
        k = self.k
        bc = lambda m: m[:, :].unsqueeze(1).to_broadcast([P, 4, P])
        gs = [(a, 2 * i + a) for a in range(2)]
        for a, g in gs:
            wait(v, s["lt"], g + 1)
            v.tensor_tensor(self.E[a][:, :, :], self.LT[a][:, :, :], bc(k.SU), ALU.mult).then_inc(s["gl"], 1)
        for a, g in gs:
            wait(v, s["gl"], g + 1)
            wait(v, s["gq"], g + 1)
            v.tensor_tensor(self.E[a][:, :, :], self.PP[a][:, 0, :, :], self.E[a][:, :, :], ALU.mult).then_inc(s["gm"], 1)
        for a, g in gs:
            wait(v, s["gm"], g + 1)
            v.tensor_tensor(self.E[a][:, :, :], self.E[a][:, :, :], beta[a].unsqueeze(2).to_broadcast([P, 4, P]), ALU.mult)\
             .then_inc(s["e"], 1)
        for a, g in gs:
            wait(v, s["e"], g + 1)
            v.tensor_tensor(self.Em[a][0][:, :, :], self.E[a][:, :, :], bc(k.LV[0]), ALU.mult).then_inc(s["em"], 1)
        for a, g in gs:
            v.tensor_tensor(self.QL[a][:, :, :], self.LT[a][:, :, :], bc(self.mask), ALU.mult).then_inc(s["ql"], 1)
        for a, g in gs:
            wait(v, s["em"], g + 1)
            v.tensor_tensor(self.XX[a][:, 1, :, :], bc(k.ident), self.Em[a][0][:, :, :], ALU.subtract).then_inc(s["x1"], 1)
            wait(v, s["p0"], g + 1)
            v.tensor_tensor(self.XX[a][:, 0, :, :], bc(k.ident), self.PP[a][:, 0, :, :], ALU.subtract).then_inc(s["xx"], 1)
        for a, g in gs:
            wait(v, s["ql"], g + 1)
            v.tensor_tensor(self.QL[a][:, :, :], self.PP[a][:, 1, :, :], self.QL[a][:, :, :], ALU.mult).then_inc(s["qm"], 1)

    def levels(self, v, s, i, lo=1, hi=LEVELS):
        gs = [(a, 2 * i + a) for a in range(2)]
        for l in range(lo, hi):
            for a, g in gs:
                if l == 1:
                    wait(v, s["x1"], g + 1)
                wait(v, s["xx"], self.at(i, a, l - 1))
                wait(v, s["p"], self.at(i, a, l - 1, LEVELS - 1))
                w = 0 if l < LEVELS - 1 else 1
                v.tensor_tensor(self.XX[a][:, w:2, :, :], self.XX[a][:, w:2, :, :], self.PP[a][:, w:2, :, :], ALU.subtract)\
                 .then_inc(s["xx"], 1)


def core_consts(k, pool, made):
    n = 0

    def done(ins):
        nonlocal n
        n += 1
        ins.then_inc(made, 1)
        pool.wait_ge(made, n)

    done(pool.memset(k.U[:, :], 1.0))
    done(pool.affine_select(out=k.U[:, :], in_=k.U[:, :], compare_op=ALU.is_ge, fill=0.0, base=0, pattern=[[1, P]], channel_multiplier=-1))
    done(pool.memset(k.U[0:T, T:P], 0.0))
    done(pool.affine_select(out=k.SU[:, :], in_=k.U[:, :], compare_op=ALU.not_equal, fill=0.0, base=0, pattern=[[1, P]], channel_multiplier=-1))
    done(pool.memset(k.SL[:, :], 1.0))
    done(pool.affine_select(out=k.SL[:, :], in_=k.SL[:, :], compare_op=ALU.is_ge, fill=0.0, base=-1, pattern=[[-1, P]], channel_multiplier=1))
    done(pool.memset(k.SL[T:P, 0:T], 0.0))
    for l in range(LEVELS):
        b = 2 ** l
        done(pool.memset(k.LV[l][:, :], 1.0))
        v4 = k.LV[l][:, :].rearrange("p (n h c) -> p n h c", h=2, c=b)
        done(pool.memset(v4[:, :, 0, :], 0.0))
        done(pool.affine_select(out=v4, in_=v4, compare_op=ALU.is_ge, fill=0.0, base=0,
                                pattern=[[-2 * b, P // (2 * b)], [0, 2], [0, b]], channel_multiplier=1))
        done(pool.affine_select(out=v4, in_=v4, compare_op=ALU.is_ge, fill=0.0, base=b - 1,
                                pattern=[[2 * b, P // (2 * b)], [0, 2], [0, b]], channel_multiplier=-1))


def softplus_vector(v, sem, y, w, p, out):
    n = 0

    def step(ins):
        nonlocal n
        n += 1
        ins.then_inc(sem, 1)
        v.wait_ge(sem, n)

    step(v.tensor_scalar(w, y, 2.0, None, ALU.add))
    step(v.reciprocal(w, w))
    step(v.tensor_tensor(y, y, w, ALU.mult))
    step(v.tensor_tensor(w, y, y, ALU.mult))
    step(v.tensor_scalar(p, w, 1.0 / 13, None, ALU.mult))
    for i in (11, 9, 7, 5, 3):
        step(v.scalar_tensor_tensor(out=p, in0=p, scalar=1.0 / i, in1=w, op0=ALU.add, op1=ALU.mult))
    step(v.scalar_tensor_tensor(out=p, in0=p, scalar=1.0, in1=y, op0=ALU.add, op1=ALU.mult))
    step(v.scalar_tensor_tensor(out=out, in0=p, scalar=2.0, in1=out, op0=ALU.mult, op1=ALU.add))


def delta0_sems(k):
    s = {n: k.sem("a1_" + n) for n in ("ldw", "wt", "wc", "sq", "ss", "rn", "rk", "rt", "rtc", "wk", "v", "vc", "g1", "g2", "sp",
                                       "g3", "g4", "mz")}
    for n in CORE_SEMS + ("cp", "cv", "oq", "oqs", "y", "lb", "w4", "xa", "x1a"):
        s[n] = k.counted("a1_" + n)
    s["n"] = norm_sems(k, "a1n")
    return s


def stage_delta0(k, s):
    nc, d = k.nc, k.dram
    ctx = ExitStack()
    sb = lambda n, s, dt=F32: k.sb("a1_" + n, s, dt, ctx)
    NG = NT // 4
    W = sb("W", [P, 2, D])
    WT = sb("WT", [P, 2, D])
    Wab = sb("Wab", [P, 2])
    alog = sb("alog", [P, 1])
    dtb = sb("dtb", [P, 1])
    sq = sb("sq", [P, NT, D])
    ss = sb("ss", [P, NT])
    rk = sb("rk", [P, NT, D])
    WR = sb("WR", [P, 2, NT * P])
    V = sb("V", [P, NT, D])
    gb = sb("gb", [P, 2, NT])
    t1 = sb("t1", [P, NT])
    t2 = sb("t2", [P, NT])
    t3 = sb("t3", [P, NT])
    t4 = sb("t4", [P, NT])
    ld = sb("ld", [P, NT])
    beta = sb("beta", [P, NT])
    two = lambda n, sh: [sb(f"{n}{a}", sh) for a in range(2)]
    wr, ldg, beg = two("wr", [P, 2, 4, P]), two("ldg", [P, 4]), two("beg", [P, 4])
    ug, vg, oqs = two("ug", [P, 4, D]), two("vg", [P, 4, D]), two("oqs", [P, 4, P])
    core = Core(k, "a1c", ctx, True)
    flat = lambda t: t[:, :, :].rearrange("p a b -> p (a b)")
    Gp, Qp, T1, Wp = core.PP[0][:, 0], core.PP[0][:, 1], core.T1[0], core.W[0]
    PP, Sm = core.PP[1], flat(core.W[1])

    with nc.Block() as block:
        @block.sync
        def _(sp):
            sp.dma_start(W[:, 0, :], d["L0_attn_W_write"]).then_inc(s["ldw"], 16)
            sp.dma_start(W[:, 1, :], d["L0_attn_W_read"]).then_inc(s["ldw"], 16)
            sp.dma_start(Wab[:, 0:1], d["L0_attn_W_alpha"].rearrange("h d -> d h")).then_inc(s["ldw"], 16)
            sp.dma_start(Wab[:, 1:2], d["L0_attn_W_beta"].rearrange("h d -> d h")).then_inc(s["ldw"], 16)
            sp.dma_start(alog[:, :], d["L0_attn_A_log"].partition_broadcast(P)).then_inc(s["ldw"], 16)
            sp.dma_start(dtb[:, :], d["L0_attn_dt_bias"].partition_broadcast(P)).then_inc(s["ldw"], 16)

        @block.gpsimd
        def _(pool):
            norm_pool(k, pool, s["n"])
            pool.wait_ge(s["ss"], 2)
            pool.tensor_tensor(ss[:, :], ss[:, :], k.half[:, 0:NT], ALU.pow).then_inc(s["rn"], 1)
            with pool.Fori(0, NG // 2) as i:
                core.parts(pool, s, i)

        @block.scalar
        def _(act):
            act.wait_ge(s["wt"], 1)
            act.activation(flat(WT), Sm[:, 0:2 * D], ACT.Copy).then_inc(s["wc"], 1)
            norm_scalar(k, act, s["n"], [flat(Gp), flat(Qp)])
            for c in range(NG):
                act.wait_ge(s["rt"], c + 1)
                act.activation(WR[:, 1, 512 * c:512 * c + 512], flat((T1, Wp)[c % 2]), ACT.Copy).then_inc(s["rtc"], 1)
            act.wait_ge(s["g1"], 1)
            act.activation(t2[:, :], t1[:, :], ACT.Abs).then_inc(s["g2"], 1)
            act.wait_ge(s["g2"], 1)
            act.activation(t2[:, :], t2[:, :], ACT.Exp, scale=-1.0).then_inc(s["g2"], 1)
            act.activation(beta[:, :], gb[:, 1, :], ACT.Exp, scale=-1.0).then_inc(s["g3"], 1)
            act.activation(alog[:, :], alog[:, :], ACT.Exp).then_inc(s["g3"], 1)
            act.wait_ge(s["wk"], 1)
            act.wait_ge(s["vc"], NT)
            with act.Fori(0, NG // 2) as i:
                gs = [(a, 2 * i + a) for a in range(2)]
                for a, g in gs:
                    wait(act, s["y"], g - 1)
                    act.activation(wr[a][:, :, :, :].rearrange("p w j t -> p w (j t)"), WR[:, :, bass.ds(g * 512, 512)], ACT.Copy).then_inc(s["cp"], 1)
                core.decays(act, s, i)
                for a, g in gs:
                    wait(act, s["u"], g - 1)
                    act.activation(vg[a][:, :, :], V[:, bass.ds(4 * g, 4), :], ACT.Copy).then_inc(s["cv"], 1)
                core.copies(act, s, i)
                for a, g in gs:
                    wait(act, s["oq"], g + 1)
                    act.activation(oqs[a][:, :, :], core.W[a][:, :, :], ACT.Copy).then_inc(s["oqs"], 1)

        @block.vector
        def _(v):
            norm_vector(k, v, s["n"])
            v.wait_ge(s["n"]["norm"], NT)
            v.tensor_tensor(sq[:, :, :], k.hn[:, :, :], k.hn[:, :, :], ALU.mult).then_inc(s["sq"], 1)
            v.wait_ge(s["sq"], 1)
            v.tensor_reduce(ss[:, :], sq[:, :, :], AXX, ALU.add).then_inc(s["ss"], 1)
            v.wait_ge(s["ss"], 1)
            v.tensor_scalar(ss[:, :], ss[:, :], 1e-24, None, ALU.max).then_inc(s["ss"], 1)
            v.wait_ge(s["rn"], 1)
            v.tensor_tensor(rk[:, :, :], k.hn[:, :, :], ss[:, :].unsqueeze(2).to_broadcast([P, NT, D]), ALU.mult).then_inc(s["rk"], 1)
            v.memset(WR[:, 0, :], 0.0).then_inc(s["mz"], 1)
            for c in range(NT // 2):
                v.wait_ge(s["v"], c + 1)
                v.tensor_copy(V[:, 2 * c:2 * c + 2, :], (PP[:, 0], PP[:, 1])[c % 2][:, 0:2, :]).then_inc(s["vc"], 1)
                v.tensor_copy(gb[:, :, 2 * c:2 * c + 2], (PP[:, 0], PP[:, 1])[c % 2][:, 2, 0:4].rearrange("p (j w) -> p w j", w=2)).then_inc(s["vc"], 1)
            v.wait_ge(s["vc"], NT)
            v.tensor_scalar(t1[:, :], gb[:, 0, :], dtb[:, 0:1], None, ALU.add).then_inc(s["g1"], 1)
            v.wait_ge(s["g1"], 1)
            v.tensor_scalar(t3[:, :], t1[:, :], 0.0, None, ALU.max).then_inc(s["g1"], 1)
            v.wait_ge(s["g3"], 2)
            v.tensor_scalar(beta[:, :], beta[:, :], 1.0, None, ALU.add).then_inc(s["g4"], 1)
            v.wait_ge(s["g4"], 1)
            v.reciprocal(beta[:, :], beta[:, :]).then_inc(s["g4"], 1)
            v.wait_ge(s["g2"], 2)
            v.wait_ge(s["g1"], 2)
            softplus_vector(v, s["sp"], t2[:, :], t1[:, :], t4[:, :], t3[:, :])
            v.tensor_scalar(ld[:, :], t3[:, :], alog[:, 0:1], -1.0, ALU.mult, ALU.mult).then_inc(s["g4"], 1)
            v.wait_ge(s["mz"], 1)
            v.wait_ge(s["rtc"], NG)
            v.tensor_copy(WR[:, 0, :].rearrange("p (b t) -> p b t", t=T)[:, :, 1:T],
                          WR[:, 1, :].rearrange("p (b t) -> p b t", t=T)[:, :, 0:T - 1]).then_inc(s["wk"], 1)
            v.wait_ge(s["g4"], 3)
            v.wait_ge(s["n"]["turned"], NG)
            with v.Fori(0, NG // 2) as i:
                gs = [(a, 2 * i + a) for a in range(2)]
                for a, g in gs:
                    v.tensor_copy(ldg[a][:, :], ld[:, bass.ds(4 * g, 4)]).then_inc(s["lb"], 1)
                    v.tensor_copy(beg[a][:, :], beta[:, bass.ds(4 * g, 4)]).then_inc(s["lb"], 1)
                wait(v, s["lb"], 4 * i + 4)
                core.spread(v, s, i, [t[:, :] for t in ldg])
                core.vector(v, s, i, [t[:, :] for t in beg])
                core.levels(v, s, i)
                for a, g in gs:
                    xs = k.x[:, bass.ds(4 * g, 4), :]
                    v.tensor_tensor(xs, xs, k.hn[:, bass.ds(4 * g, 4), :], ALU.add).then_inc(s["xa"], 1)
                    wait(v, s["w4"], g + 1)
                    v.tensor_tensor(ug[a][:, :, :], core.W[a][:, :, :], beg[a][:, :].unsqueeze(2).to_broadcast([P, 4, D]), ALU.mult).then_inc(s["u"], 1)
                for a, g in gs:
                    xs = k.x[:, bass.ds(4 * g, 4), :]
                    wait(v, s["xa"], g + 1)
                    wait(v, s["y"], g + 1)
                    v.tensor_tensor(xs, xs, core.PP[a][:, 0, :, :], ALU.add).then_inc(s["x1a"], 1)

        @block.tensor
        def _(pe):
            pe.wait_ge(s["ldw"], 96)
            for i in range(2):
                mm = pe.transpose(Sm[:, P * i:P * i + P], W[:, i, :], k.ident[:, :])
            mm.then_inc(s["wt"], 1)
            norm_tensor(k, pe, s["n"], [flat(Gp), flat(Qp)])
            pe.wait_ge(s["rk"], 1)
            for c in range(NG):
                if c >= 2:
                    pe.wait_ge(s["rtc"], c - 1)
                for j in range(4):
                    mm = pe.transpose((T1, Wp)[c % 2][:, j, :], rk[:, 4 * c + j, :], k.ident[:, :])
                mm.then_inc(s["rt"], 1)
            pe.wait_ge(s["wc"], 1)
            pe.wait_ge(s["n"]["copied"], NG)
            for c in range(NT // 2):
                if c >= 2:
                    pe.wait_ge(s["vc"], 2 * (c - 1))
                bank = (PP[:, 0], PP[:, 1])[c % 2]
                for j in range(2):
                    h = k.hT[:, P * (2 * c + j):P * (2 * c + j) + P]
                    pe.matmul(bank[:, j, :], h, WT[:, 0, :], start=True, stop=True)
                    mm = pe.matmul(bank[:, 2, 2 * j:2 * j + 2], h, Wab[:, :], start=True, stop=True)
                mm.then_inc(s["v"], 1)
            pe.wait_ge(s["rtc"], NG)
            pe.wait_ge(s["vc"], NT)
            pe.wait_ge(s["wk"], 1)
            with pe.Fori(0, NG // 2) as i:
                gs = [(a, 2 * i + a) for a in range(2)]
                core.sums(pe, s, i)
                for a, g in gs:
                    wait(pe, s["cp"], g + 1)
                    wait(pe, s["x1a"], g - 1)
                    for j in range(4):
                        pe.matmul(core.PP[a][:, 0, j, :], wr[a][:, 0, j, :], wr[a][:, 0, j, :], start=True, stop=True)
                        mm = pe.matmul(core.PP[a][:, 1, j, :], wr[a][:, 0, j, :], wr[a][:, 1, j, :], start=True, stop=True)
                    mm.then_inc(s["gq"], 1)
                core.solve(pe, s, i)
                for a, g in gs:
                    wait(pe, s["xx"], core.at(i, a, LEVELS - 1))
                    wait(pe, s["cv"], g + 1)
                    for j in range(4):
                        mm = pe.matmul(core.W[a][:, j, :], core.XX[a][:, 1, j, :], vg[a][:, j, :], start=True, stop=True)
                    mm.then_inc(s["w4"], 1)
                for a, g in gs:
                    wait(pe, s["u"], g + 1)
                    for j in range(4):
                        mm = pe.matmul(core.W[a][:, j, :], ug[a][:, j, :], core.QL[a][:, j, :], start=True, stop=True)
                    mm.then_inc(s["oq"], 1)
                for a, g in gs:
                    wait(pe, s["oqs"], g + 1)
                    for j in range(4):
                        mm = pe.matmul(core.PP[a][:, 0, j, :], oqs[a][:, j, :], WT[:, 1, :], start=True, stop=True)
                    mm.then_inc(s["y"], 1)
    ctx.close()


E8 = 8
MOE_SEMS = ("up", "ge", "dn", "ax")
ROUTE_SEMS = ("lg", "r", "re")


def route_vector(k, v, s, logits, bias, r):
    bc = lambda a: a.unsqueeze(2).to_broadcast([P, NT, E8])
    n = 0

    def step(ins):
        nonlocal n
        n += 1
        ins.then_inc(s["r"], 1)
        v.wait_ge(s["r"], n)

    v.wait_ge(s["lg"], 1)
    if bias is not None:
        step(v.tensor_tensor(r.p[:, :, :], logits, bias[:, :].unsqueeze(1).to_broadcast([P, NT, E8]), ALU.add))
    else:
        step(v.tensor_copy(r.p[:, :, :], logits))
    step(v.tensor_reduce(r.m[:, :], r.p[:, :, :], AXX, ALU.max))
    step(v.tensor_tensor(r.p[:, :, :], r.p[:, :, :], bc(r.m[:, :]), ALU.subtract))
    v.engine_nop().then_inc(s["re"], 1)
    v.wait_ge(s["re"], 2)
    step(v.tensor_reduce(r.m[:, :], r.p[:, :, :], AXX, ALU.add))
    step(v.reciprocal(r.m[:, :], r.m[:, :]))
    step(v.tensor_tensor(r.p[:, :, :], r.p[:, :, :], bc(r.m[:, :]), ALU.mult))
    for i in range(2):
        step(v.tensor_reduce(r.m[:, :], r.p[:, :, :], AXX, ALU.max))
        step(v.tensor_tensor(r.c[:, :, :], r.p[:, :, :], bc(r.m[:, :]), ALU.is_equal))
        step(v.tensor_tensor(r.c[:, :, :], r.c[:, :, :], k.rank[:, :].unsqueeze(1).to_broadcast([P, NT, E8]), ALU.mult))
        step(v.tensor_reduce(r.m[:, :], r.c[:, :, :], AXX, ALU.max))
        step(v.tensor_tensor(r.c[:, :, :], r.c[:, :, :], bc(r.m[:, :]), ALU.is_equal))
        if i == 0:
            step(v.tensor_tensor(r.comb[:, :, :], r.p[:, :, :], r.c[:, :, :], ALU.mult))
            step(v.tensor_scalar(r.c[:, :, :], r.c[:, :, :], 4.0, None, ALU.mult))
            step(v.tensor_tensor(r.p[:, :, :], r.p[:, :, :], r.c[:, :, :], ALU.subtract))
        else:
            step(v.tensor_tensor(r.c[:, :, :], r.p[:, :, :], r.c[:, :, :], ALU.mult))
            step(v.tensor_tensor(r.comb[:, :, :], r.comb[:, :, :], r.c[:, :, :], ALU.add))


def route_scalar(k, act, s, r):
    act.wait_ge(s["re"], 1)
    act.activation(r.p[:, :, :], r.p[:, :, :], ACT.Exp).then_inc(s["re"], 1)


def route_tensor(k, pe, s, logits, w):
    for n in range(NT):
        mm = pe.matmul(logits[:, n, :], k.hT[:, P * n:P * n + P], w[:, :], start=True, stop=True)
    mm.then_inc(s["lg"], 1)


class Moe:

    def __init__(self, k, tag, ctx, FB, up, down, func):
        sb = lambda n, sh, dt=F32: k.sb(f"{tag}_{n}", sh, dt, ctx)
        self.k, self.FB, self.up, self.down, self.func = k, FB, up, down, func
        self.H = [sb(f"H{i}", [P, FB, 512]) for i in range(2)]
        self.p, self.c, self.comb = (sb(n, [P, NT, E8]) for n in ("p", "c", "comb"))
        self.m = sb("m", [P, NT])
        self.U = [k.ps(f"{tag}_U{i}", [P, 512], F32, ctx) for i in range(4)]
        self.Dn = [k.ps(f"{tag}_D{i}", [P, 4, D], F32, ctx) for i in range(2)]

    def tensor(self, pe, s):
        k, FB = self.k, self.FB

        def ups(c, e):
            for f in range(FB):
                g = FB * (E8 * c + e) + f
                wait(pe, s["ge"], g - 3)
                pe.matmul(self.U[(FB * e + f) % 4][:, :], self.up(e, f), k.hT[:, bass.ds(512 * c, 512)], start=True, stop=True)\
                  .then_inc(s["up"], 1)

        def downs(c, e):
            q = E8 * c + e
            wait(pe, s["ge"], FB * (q + 1))
            wait(pe, s["ax"], 4 * (q - 1))
            for j in range(4):
                for f in range(FB):
                    mm = pe.matmul(self.Dn[e % 2][:, j, :], self.H[e % 2][:, f, P * j:P * j + P], self.down(e, f),
                                   start=(f == 0), stop=(f == FB - 1))
            mm.then_inc(s["dn"], 1)

        with pe.Fori(0, NT // 4) as c:
            ups(c, 0)
            for e in range(E8):
                if e + 1 < E8:
                    ups(c, e + 1)
                downs(c, e)

    def scalar(self, act, s):
        with act.Fori(0, NT // 4) as c:
            for e in range(E8):
                for f in range(self.FB):
                    wait(act, s["up"], self.FB * (E8 * c + e) + f + 1)
                    if f == 0:
                        wait(act, s["dn"], E8 * c + e - 1)
                    act.activation(self.H[e % 2][:, f, :], self.U[(self.FB * e + f) % 4][:, :], self.func)\
                       .then_inc(s["ge"], 1)

    def vector(self, v, s):
        k = self.k
        with v.Fori(0, NT // 4) as c:
            for e in range(E8):
                q = E8 * c + e
                for j in range(4):
                    if j == 0:
                        wait(v, s["dn"], q + 1)
                    if e > 0:
                        wait(v, s["ax"], 4 * q - 3 + j)
                    xs = k.x[:, bass.ds(4 * c + j, 1), :].rearrange("p o d -> p (o d)")
                    v.scalar_tensor_tensor(out=xs, in0=self.Dn[e % 2][:, j, :],
                                           scalar=self.comb[:, bass.ds(4 * c + j, 1), e:e + 1].rearrange("p o e -> p (o e)"),
                                           in1=xs, op0=ALU.mult, op1=ALU.add).then_inc(s["ax"], 1)


def moe0_sems(k):
    s = {n: k.sem("a2_" + n) for n in ROUTE_SEMS + ("ldr", "lu", "ldd", "wt", "wc")}
    for n in MOE_SEMS:
        s[n] = k.counted("a2_" + n)
    s["n"] = norm_sems(k, "a2n")
    return s


def stage_moe0(k, s):
    nc, d = k.nc, k.dram
    ctx = ExitStack()
    sb = lambda n, s, dt=F32: k.sb("a2_" + n, s, dt, ctx)
    F = 512
    FB = F // P
    up = sb("up", [P, E8 * FB, D])
    dn = sb("dn", [P, E8, F])
    upT = sb("upT", [P, E8 * FB, P])
    dnT = sb("dnT", [P, E8 * FB, P])
    Wr = sb("Wr", [P, E8])
    br = sb("br", [P, E8])
    m = Moe(k, "a2", ctx, FB, lambda e, f: upT[:, FB * e + f, :], lambda e, f: dnT[:, FB * e + f, :], ACT.Gelu)
    LG = k.ps("a2_L", [P, NT, E8], F32, ctx)
    banks = [m.Dn[i][:, :, :].rearrange("p j d -> p (j d)") for i in range(2)]

    with nc.Block() as block:
        @block.sync
        def _(sp):
            sp.dma_start(up[:, :, :], d["L0_ffn_expert_up"].rearrange("e (f p) d -> p (e f) d", p=P)).then_inc(s["lu"], 16)
            sp.dma_start(dn[:, :, :], d["L0_ffn_expert_down"].rearrange("e d f -> d e f")).then_inc(s["ldd"], 16)
            sp.dma_start(Wr[:, :], d["L0_ffn_router_w"]).then_inc(s["ldr"], 16)
            sp.dma_start(br[:, :], d["L0_ffn_router_b"].partition_broadcast(P)).then_inc(s["ldr"], 16)

        @block.gpsimd
        def _(pool):
            norm_pool(k, pool, s["n"])

        def turn(i):
            if i < E8:
                return [up[:, FB * i + f, :] for f in range(FB)], upT[:, FB * i:FB * i + FB, :]
            e = i - E8
            return [dn[:, e, P * f:P * f + P] for f in range(FB)], dnT[:, FB * e:FB * e + FB, :]

        @block.scalar
        def _(act):
            norm_scalar(k, act, s["n"], banks)
            route_scalar(k, act, s, m)
            act.wait_ge(s["wc"], 2 * E8)
            m.scalar(act, s)

        @block.vector
        def _(v):
            norm_vector(k, v, s["n"])
            for i in range(2 * E8):
                v.wait_ge(s["wt"], i + 1)
                v.tensor_copy(turn(i)[1].rearrange("p f d -> p (f d)"), m.U[i % 4][:, :]).then_inc(s["wc"], 1)
            v.wait_ge(s["ldr"], 32)
            route_vector(k, v, s, LG[:, :, :], br, m)
            v.wait_ge(s["n"]["copied"], NT // 4)
            m.vector(v, s)

        @block.tensor
        def _(pe):
            pe.wait_ge(s["lu"], 16)
            for i in range(2 * E8):
                if i == E8:
                    pe.wait_ge(s["ldd"], 16)
                if i >= 4:
                    pe.wait_ge(s["wc"], i - 3)
                for f, w in enumerate(turn(i)[0]):
                    mm = pe.transpose(m.U[i % 4][:, P * f:P * f + P], w, k.ident[:, :])
                mm.then_inc(s["wt"], 1)
            norm_tensor(k, pe, s["n"], banks)
            pe.wait_ge(s["n"]["copied"], NT // 4)
            pe.wait_ge(s["ldr"], 32)
            route_tensor(k, pe, s, LG, Wr)
            pe.wait_ge(s["wc"], 2 * E8)
            m.tensor(pe, s)
    ctx.close()


def xattn1_sems(k):
    s = {n: k.sem("a3_" + n) for n in ("ldw", "ld0", "ld1", "wt", "wc", "gh", "ghc", "n2", "n3", "n3b", "qt", "qtc")}
    for n in ("z", "gm", "gt", "xn", "lat", "tt", "xt", "ltc", "qa", "qb", "xb", "as", "am", "m1", "mt", "mx", "sc", "exp", "pv",
              "acc", "pvc", "tot", "rc", "on", "y", "x"):
        s[n] = k.counted("a3_" + n)
    s["n"] = norm_sems(k, "a3n")
    return s


def stage_xattn1(k, s):
    nc, d = k.nc, k.dram
    H, DH = 8, 64
    HQ = H * T
    ISCALE = DH ** 0.5
    SK = S + T
    NU = 14
    TURN = 2
    OUT = 5
    NB = 8
    ctx = ExitStack()
    sb = lambda n, s, dt=F32: k.sb("a3_" + n, s, dt, ctx)
    C = [sb(f"C{i}", [P, NK, D]) for i in range(2)]
    XN = [sb(f"XN{i}", [P, NK + 1, D]) for i in range(2)]
    XT = [sb(f"XT{i}", [P, SK]) for i in range(2)]
    XTb = sb("XTb", [P, SK], BF16)
    QT = sb("QT", [P, B, H, T])
    QA = [sb(f"QA{i}", [P, H, T]) for i in range(2)]
    QAb = sb("QAb", [P, H, T], BF16)
    negm = [sb(f"negm{i}", [4, 4, P], BF16) for i in range(2)]
    acc = [sb(f"acc{i}", [P, HQ]) for i in range(2)]
    gmB, bmB, glB, blB = (sb(n, [P, D]) for n in ("gm", "bm", "gl", "bl"))
    GH = sb("GH", [P, H, D])
    HH = sb("HH", [P, H, D])
    mx = sb("mx", [P, 4, 4])
    mxm = sb("mxm", [P, 4])
    pvs = sb("pvs", [P, HQ])
    rs = sb("rs", [P, HQ])
    on = sb("on", [P, HQ])
    k_mv, k_rs = k.cmv, k.crstd
    SC = [k.ps(f"a3_SC{i}", [P, 2 * HQ], F32, ctx) for i in range(2)]
    PV = k.ps("a3_PV", [P, HQ], F32, ctx)
    A = [k.ps(f"a3_A{i}", [P, 512], F32, ctx) for i in range(2)]
    M = k.ps("a3_M", [P, 512], F32, ctx)
    wctx = ExitStack()
    wsb = lambda n, s: k.sb("a3_" + n, s, F32, wctx)
    Wq = wsb("Wq", [P, H * DH])
    Wkv = wsb("Wkv", [P, 2 * H * DH])
    WT = wsb("WT", [P, 3, 4, D])
    Wo = wsb("Wo", [P, 4, D])
    wctx.close()
    PT = [sb(f"PT{i}", [P, 2 * HQ]) for i in range(4)]

    def tiles(u):
        return (2 * u, 2 * u + 1) if u < 6 else (6 + u,)

    def top_units(u):
        n = NB - TURN - 2
        return range(NU * (u - TURN - 2) // n, NU * (u - TURN - 1) // n) if u >= TURN + 2 else range(0)

    def rows(j):
        return wcols(j) if j < NK else T

    def col(j):
        return P * j if j < NK else S

    def keyrange(c):
        return 512 * c, min(512, SK - 512 * c)

    with nc.Block() as block:
        @block.sync
        def _(sp):
            for t, n in ((Wq, "Wq"), (Wkv, "Wkv")):
                sp.dma_start(t[:, :], d["L1_xattn_" + n]).then_inc(s["ldw"], 16)
            sp.dma_start(Wo[:, :, :], d["L1_xattn_Wout"].rearrange("(j p) d -> p j d", p=P)).then_inc(s["ldw"], 16)
            for t, n in ((gmB, "gm"), (bmB, "bm"), (glB, "gl"), (blB, "bl")):
                sp.dma_start(t[:, :], d["L1_xattn_" + n].partition_broadcast(P)).then_inc(s["ldw"], 16)

            def load(b, a):
                wait(sp, s["xn"], b - 1)
                sp.dma_start(C[a][:, 0:KF, :], d["ctx_1024"][bass.ds(b, 1), 0:KF * P, :].rearrange("o (p j) d -> p (o j) d", p=P))\
                  .then_inc(s[f"ld{a}"], 16)
                sp.dma_start(C[a][0:SR, KF, :], d["ctx_1024"][bass.ds(b, 1), KF * P:S, :].rearrange("o p d -> p (o d)"))\
                  .then_inc(s[f"ld{a}"], 16)

            load(0, 0)
            load(1, 1)
            with sp.Fori(0, B // 2 - 1) as i:
                load(2 * i + 2, 0)
                load(2 * i + 3, 1)

        @block.gpsimd
        def _(pool):
            norm_pool(k, pool, s["n"])
            pool.wait_ge(s["n2"], NT + 1)
            pool.tensor_tensor(k.rstd[:, :], k.rstd[:, :], k.half[:, 0:NT], ALU.pow).then_inc(s["n3"], 1)
            pool.wait_ge(s["ldw"], 16 * 7)

            def gain(b, a):
                wait(pool, s["z"], NK * (b + 1))
                for lo, hi, m in ((0, KF, P), (KF, NK, SR)):
                    pool.tensor_tensor(C[a][0:m, lo:hi, :], C[a][0:m, lo:hi, :], gmB[0:m, :].unsqueeze(1).to_broadcast([m, hi - lo, D]),
                                       ALU.mult).then_inc(s["gm"], 1)

            def shift(b, a):
                wait(pool, s["gm"], 2 * b + 2)
                wait(pool, s["pv"], NB * (b - 1))
                for lo, hi, m in ((0, KF, P), (KF, NK, SR)):
                    ins = pool.tensor_tensor(XN[a][0:m, lo:hi, :], C[a][0:m, lo:hi, :], bmB[0:m, :].unsqueeze(1).to_broadcast([m, hi - lo, D]),
                                             ALU.add)
                    ins.then_inc(s["gt" if lo == 0 else "xn"], 1)

            def sums(b, a):
                n = 0
                for u in range(NB):
                    wait(pool, s["exp"], NB * b + u + 1)
                    for i, j in enumerate(tiles(u)):
                        if j == 0:
                            continue
                        m = rows(j)
                        if n == 0:
                            wait(pool, s["tot"], b - 1)
                            first = PT[0][:, 0:HQ]
                        else:
                            wait(pool, s["acc"], NK * b + n)
                            first = acc[a][0:m, :]
                        pool.tensor_tensor(acc[a][0:m, :], first, PT[u % 4][0:m, HQ * i:HQ * i + HQ], ALU.add).then_inc(s["acc"], 1)
                        n += 1

            def step(b, a, one, two):
                if one:
                    shift(b + 1, 1 - a)
                sums(b, a)
                if two:
                    gain(b + 2, a)

            gain(0, 0)
            shift(0, 0)
            gain(1, 1)
            step(0, 0, True, True)
            with pool.Fori(0, B // 2 - 2) as i:
                step(2 * i + 1, 1, True, True)
                step(2 * i + 2, 0, True, True)
            step(B - 3, 1, True, True)
            step(B - 2, 0, True, False)
            step(B - 1, 1, False, False)

        def added(b, u):
            if u < 4:
                return NK * (b - 1) + (9, 11, 12, 13)[u]
            return NK * b + 2 * (u - 4) + 1

        @block.scalar
        def _(act):
            for c in range(3):
                act.wait_ge(s["wt"], c + 1)
                act.activation(WT[:, c, :, :].rearrange("p j d -> p (j d)"), (M, PV, M)[c][:, :], ACT.Copy).then_inc(s["wc"], 1)
            for c in range(4):
                act.wait_ge(s["gh"], c + 1)
                dst = (GH, HH)[c // 2][:, c % 2:H:2, :]
                act.activation(dst, SC[c // 2][:, HQ * (c % 2):HQ * (c % 2) + HQ].rearrange("p (i d) -> p i d", d=D),
                               ACT.Copy, scale=ISCALE if c < 2 else 1.0).then_inc(s["ghc"], 1)
            norm_scalar(k, act, s["n"], A)
            for g in range(H * 4):
                h, c = g % H, g // H
                act.wait_ge(s["qt"], g + 1)
                act.activation(QT[:, 8 * c:8 * c + 8, h, :], (PV, M)[g % 2][:, :].rearrange("p (b t) -> p b t", t=T), ACT.Copy)\
                   .then_inc(s["qtc"], 1)

            def turned(b, a, c):
                c0, n = 512 * c, (512 if c < 3 else SR)
                wait(act, s["tt"], 4 * b + c + 1)
                act.activation(XT[a][:, c0:c0 + n], A[c % 2][:, 0:n], ACT.Copy).then_inc(s["xt"], 1)
                if c == 0:
                    act.activation(XT[a][:, S:SK], k.hT[:, bass.ds(b * T, T)], ACT.Copy).then_inc(s["ltc"], 1)

            def probs(b, a, u):
                g = NB * b + u
                wait(act, s["sc"], g + 1)
                wait(act, s["pv"], g - 3)
                wait(act, s["acc"], added(b, u))
                m = rows(tiles(u)[0])
                n = HQ * len(tiles(u))
                act.activation(PT[u % 4][0:m, 0:n], SC[u % 2][0:m, 0:n], ACT.Exp).then_inc(s["exp"], 1)

            def step(b, a, more):
                for u in range(NB):
                    probs(b, a, u)
                    if more and TURN <= u < TURN + 2:
                        turned(b + 1, 1 - a, 2 * (u - TURN))
                        turned(b + 1, 1 - a, 2 * (u - TURN) + 1)

            for c in range(4):
                turned(0, 0, c)
            step(0, 0, True)
            with act.Fori(0, B // 2 - 1) as i:
                step(2 * i + 1, 1, True)
                step(2 * i + 2, 0, True)
            step(B - 1, 1, False)

        @block.vector
        def _(v):
            norm_vector(k, v, s["n"])
            v.wait_ge(s["n"]["norm"], NT)
            for n in range(NT):
                v.bn_stats(k.st6[:, n, :], k.hn[:, n, :]).then_inc(s["n2"], 1)
            v.wait_ge(s["n2"], NT)
            for n in range(NT):
                mm = v.bn_aggr(k.mv[:, n, :], k.st6[:, n, :])
                mm.then_inc(s["n3b"], 1)
            v.wait_ge(s["n3b"], NT)
            v.tensor_scalar(k.rstd[:, :], k.mv[:, :, 1], LN_EPS, None, ALU.add).then_inc(s["n2"], 1)
            v.wait_ge(s["n3"], 1)
            for n in range(NT):
                v.tensor_scalar(k.hn[:, n, :], k.hn[:, n, :], k.mv[:, n, 0:1], k.rstd[:, n:n + 1], ALU.subtract, ALU.mult)\
                 .then_inc(s["n3b"], 1)
            v.wait_ge(s["n3b"], 2 * NT)
            v.wait_ge(s["ldw"], 16 * 7)
            v.tensor_tensor(k.hn[:, :, :], k.hn[:, :, :], glB[:, :].unsqueeze(1).to_broadcast([P, NT, D]), ALU.mult).then_inc(s["n3b"], 1)
            v.wait_ge(s["n3b"], 2 * NT + 1)
            v.tensor_tensor(k.hn[:, :, :], k.hn[:, :, :], blB[:, :].unsqueeze(1).to_broadcast([P, NT, D]), ALU.add).then_inc(s["n2"], 1)

            def norm(b, a):
                v.wait_ge(s[f"ld{a}"], 16 * (b - a) + 32)
                for j in range(NK):
                    m = wcols(j)
                    v.tensor_scalar(C[a][0:m, j, :], C[a][0:m, j, :], k_mv[0:m, bass.ds(b, 1), j, 0:1].rearrange("p o e -> p (o e)"),
                                    k_rs[0:m, bass.ds(b, 1), j:j + 1].rearrange("p o e -> p (o e)"), ALU.subtract, ALU.mult)\
                     .then_inc(s["z"], 1)

            def feed(b, a, pair):
                wait(v, s["pv"], NB * (b - 1))
                v.tensor_copy(QA[a][:, :, :], QT[:, bass.ds(b, 1), :, :].rearrange("p o h t -> p (o h) t")).then_inc(s["qa"], 1)
                v.tensor_copy(XN[a][0:T, NK, :], k.hn[T * a:T * a + T, bass.ds(pair, 1), :].rearrange("p o d -> p (o d)"))\
                 .then_inc(s["lat"], 1)
                wait(v, s["qa"], b + 1)
                wait(v, s["mx"], b)
                v.tensor_copy(QAb[:, :, :], QA[a][:, :, :]).then_inc(s["qb"], 1)
                wait(v, s["ltc"], b + 1)
                for c in range(4):
                    c0, n = keyrange(c)
                    wait(v, s["xt"], 4 * b + c + 1)
                    v.tensor_copy(XTb[:, c0:c0 + n], XT[a][:, c0:c0 + n]).then_inc(s["xb"], 1)

            def tops(b, u):
                wait(v, s["as"], NU * b + u + 1)
                if u < 12:
                    v.tensor_reduce(mx[:, u % 4, u // 4:u // 4 + 1], A[u % 2][:, :], AXX, ALU.max).then_inc(s["am"], 1)
                else:
                    p0, n = (0, 3) if u == 12 else (3, 1)
                    w = SK - 3 * 512
                    v.tensor_reduce(mx[:, p0:p0 + n, 3], A[u % 2][:, 0:n * w].rearrange("q (p s) -> q p s", s=w), AXX, ALU.max)\
                     .then_inc(s["am"], 1)

            def top(b, a):
                wait(v, s["am"], NU * (b + 1))
                v.tensor_reduce(mxm[:, :], mx[:, :, :], AXX, ALU.max).then_inc(s["m1"], 1)
                wait(v, s["mt"], b + 1)
                v.tensor_tensor(negm[a][:, :, :], M[0:4, 0:P].unsqueeze(1).to_broadcast([4, 4, P]),
                                k.negdiag[0:4, 0:4, :], ALU.mult).then_inc(s["mx"], 1)

            def copy_out(b):
                wait(v, s["pv"], NB * (b + 1))
                wait(v, s["on"], b)
                v.tensor_copy(pvs[:, :], PV[:, :]).then_inc(s["pvc"], 1)

            def final(b):
                wait(v, s["tot"], b + 1)
                wait(v, s["on"], b)
                v.reciprocal(rs[:, :], M[:, :]).then_inc(s["rc"], 1)
                wait(v, s["rc"], b + 1)
                wait(v, s["pvc"], b + 1)
                wait(v, s["y"], b)
                v.tensor_tensor(on[:, :], pvs[:, :], rs[:, :], ALU.mult).then_inc(s["on"], 1)

            def add(b, a, pair):
                wait(v, s["y"], b + 1)
                xs = k.x[T * a:T * a + T, bass.ds(pair, 1), :].rearrange("p o d -> p (o d)")
                v.tensor_tensor(xs, xs, M[T * a:T * a + T, 0:D], ALU.add).then_inc(s["x"], 1)

            def step(b, a, pair, one, two):
                if not (isinstance(b, int) and b == 0):
                    copy_out(b - 1)
                    final(b - 1)
                if one:
                    feed(b + 1, 1 - a, pair + a)
                before = top_units(OUT)[0] if one else 0
                for u in range(before):
                    tops(b + 1, u)
                if not (isinstance(b, int) and b == 0):
                    add(b - 1, 1 - a, pair + a - 1)
                if one:
                    for u in range(before, NU):
                        tops(b + 1, u)
                    top(b + 1, 1 - a)
                if two:
                    norm(b + 2, a)

            v.wait_ge(s["qtc"], 4 * H)
            norm(0, 0)
            norm(1, 1)
            feed(0, 0, 0)
            for u in range(NU):
                tops(0, u)
            top(0, 0)
            step(0, 0, 0, True, True)
            with v.Fori(0, B // 2 - 2) as i:
                step(2 * i + 1, 1, i, True, True)
                step(2 * i + 2, 0, i + 1, True, True)
            step(B - 3, 1, NT - 2, True, True)
            step(B - 2, 0, NT - 1, True, False)
            step(B - 1, 1, NT - 1, False, False)
            copy_out(B - 1)
            final(B - 1)
            add(B - 1, 1, NT - 1)

        @block.tensor
        def _(pe):
            pe.wait_ge(s["ldw"], 16 * 7)
            for c in range(3):
                if c == 2:
                    pe.wait_ge(s["wc"], 1)
                for j in range(4):
                    src = (Wq, Wkv, Wkv)[c][:, (0, 0, H * DH)[c] + P * j:(0, 0, H * DH)[c] + P * j + P]
                    mm = pe.transpose((M, PV, M)[c][:, P * j:P * j + P], src, k.ident[:, :])
                mm.then_inc(s["wt"], 1)
            pe.wait_ge(s["wc"], 3)
            for c in range(4):
                for i in range(4):
                    h = 2 * i + c % 2
                    r = slice(DH * (h % 2), DH * (h % 2) + DH)
                    o = SC[c // 2][:, HQ * (c % 2) + D * i:HQ * (c % 2) + D * i + D]
                    if c < 2:
                        mm = pe.matmul(o, WT[r, 0, h // 2, :], WT[r, 1, h // 2, :], start=True, stop=True)
                    else:
                        mm = pe.matmul(o, WT[r, 2, h // 2, :], Wo[r, h // 2, :], start=True, stop=True)
                mm.then_inc(s["gh"], 1)
            pe.wait_ge(s["n2"], NT + 2)
            norm_tensor(k, pe, s["n"], A)
            pe.wait_ge(s["n"]["copied"], 4)
            pe.wait_ge(s["ghc"], 4)
            for g in range(H * 4):
                if g >= 2:
                    pe.wait_ge(s["qtc"], g - 1)
                c = g // H
                pe.matmul((PV, M)[g % 2][:, :], GH[:, g % H, :], k.hT[:, 512 * c:512 * c + 512], start=True, stop=True).then_inc(s["qt"], 1)
            pe.wait_ge(s["qtc"], 4 * H)

            def turn(b, a, c):
                if c == 0:
                    wait(pe, s["xn"], b + 1)
                    wait(pe, s["gt"], b + 1)
                    wait(pe, s["am"], NU * b)
                elif c >= 2:
                    wait(pe, s["xt"], 4 * b + c - 1)
                for j in range(4 * c, min(4 * c + 4, NK)):
                    m = wcols(j)
                    mm = pe.transpose(A[c % 2][:, P * (j % 4):P * (j % 4) + m], XN[a][0:m, j, :], k.ident[0:m, 0:m])
                mm.then_inc(s["tt"], 1)

            def tops(b, u):
                if u == 0:
                    wait(pe, s["qb"], b + 1)
                    wait(pe, s["xb"], 4 * b + 4)
                wait(pe, s["am"], NU * b + u - 1)
                if u < 12:
                    p, c = u % 4, u // 4
                    mm = pe.matmul(A[u % 2][:, :], QAb[:, 2 * p:2 * p + 2, :], XTb[:, 512 * c:512 * c + 512], start=True, stop=True)
                else:
                    w = SK - 3 * 512
                    for i, p in enumerate((0, 1, 2) if u == 12 else (3,)):
                        mm = pe.matmul(A[u % 2][:, w * i:w * i + w], QAb[:, 2 * p:2 * p + 2, :], XTb[:, 3 * 512:SK], start=True, stop=True)
                mm.then_inc(s["as"], 1)

            def top(b):
                wait(pe, s["m1"], b + 1)
                wait(pe, s["x"], b - 1)
                pe.transpose(M[0:4, 0:P], mxm[:, :], k.ident[:, :]).then_inc(s["mt"], 1)

            def scores(b, a, u):
                if u == 0:
                    wait(pe, s["mx"], b + 1)
                    wait(pe, s["ltc"], b + 1)
                    wait(pe, s["qa"], b + 1)
                wait(pe, s["exp"], NB * b + u - 1)
                for i, j in enumerate(tiles(u)):
                    m = rows(j)
                    o = SC[u % 2][0:m, HQ * i:HQ * i + HQ]
                    pe.matmul(o, XT[a][:, col(j):col(j) + m], QA[a][:, :, :], start=True, stop=False)
                    mm = pe.matmul(o, k.onesb[0:4, 0:m], negm[a][:, :, :], start=False, stop=True)
                mm.then_inc(s["sc"], 1)

            def products(b, a, u):
                wait(pe, s["exp"], NB * b + u + 1)
                if u == 0:
                    wait(pe, s["pvc"], b)
                    wait(pe, s["lat"], b + 1)
                for i, j in enumerate(tiles(u)):
                    m = rows(j)
                    mm = pe.matmul(PV[:, :], XN[a][0:m, j, :], PT[u % 4][0:m, HQ * i:HQ * i + HQ], start=(j == 0), stop=(j == NK))
                mm.then_inc(s["pv"], 1)

            def total(b, a):
                wait(pe, s["acc"], NK * (b + 1))
                wait(pe, s["mx"], min(b + 2, B) if isinstance(b, int) else b + 2)
                pe.matmul(M[:, :], k.ones[:, :], acc[a][:, :], start=True, stop=True).then_inc(s["tot"], 1)

            def out(b, a):
                wait(pe, s["on"], b + 1)
                for h in range(H):
                    mm = pe.matmul(M[T * a:T * a + T, 0:D], on[:, T * h:T * h + T], HH[:, h, :], start=(h == 0), stop=(h == H - 1))
                mm.then_inc(s["y"], 1)

            def step(b, a, more):
                first = isinstance(b, int) and b == 0
                scores(b, a, 0)
                for u in range(NB):
                    if u + 1 < NB:
                        scores(b, a, u + 1)
                    if u == 1 and not first:
                        total(b - 1, 1 - a)
                    if more and TURN <= u < TURN + 2:
                        turn(b + 1, 1 - a, 2 * (u - TURN))
                        turn(b + 1, 1 - a, 2 * (u - TURN) + 1)
                    if u == OUT and not first:
                        out(b - 1, 1 - a)
                    for n in (top_units(u) if more else ())[0:2]:
                        tops(b + 1, n)
                    products(b, a, u)
                    for n in (top_units(u) if more else ())[2:]:
                        tops(b + 1, n)
                if more:
                    top(b + 1)

            for c in range(4):
                turn(0, 0, c)
            for u in range(NU):
                tops(0, u)
            top(0)
            step(0, 0, True)
            with pe.Fori(0, B // 2 - 1) as i:
                step(2 * i + 1, 1, True)
                step(2 * i + 2, 0, True)
            step(B - 1, 1, False)
            wait(pe, s["x"], B - 1)
            total(B - 1, 1)
            wait(pe, s["rc"], B)
            out(B - 1, 1)
    ctx.close()


def delta1_sems(k):
    s = {n: k.sem("a4_" + n) for n in ("ldw", "wt", "wc", "wf", "wfc", "pz", "xz", "xzc", "cv0", "cv1", "sl0", "sl1", "pj", "pjc", "l2",
                                       "l2s", "g1", "g2", "sp", "g3", "g4", "kz", "o1", "o1s", "ot", "otc", "y", "x")}
    for n in CORE_SEMS + ("lb", "ll", "cp", "cv", "kt", "ktc", "kx", "w4", "oo", "oc"):
        s[n] = k.counted("a4_" + n)
    s["n"] = norm_sems(k, "a4n")
    return s


def stage_delta1(k, s):
    nc, d = k.nc, k.dram
    H, DK, DV, KP_ = 4, 24, 48, 32
    KD, VD = H * DK, H * DV
    W3 = 2 * KD + 2 * VD + 2 * H
    GPAD = T + 3
    ctx = ExitStack()
    sb = lambda n, sh, dt=F32: k.sb("a4_" + n, sh, dt, ctx)
    Win = sb("Win", [P, 2, P])
    cw = sb("cw", [P, 2, 4])
    cb = sb("cb", [P, 2])
    Wp = sb("Wp", [P, W3])
    Wso = sb("Wso", [VD // 2, 2, P])
    WsoT = sb("WsoT", [P, 2, VD // 2])
    Wo = sb("Wo", [P, 2, D])
    Wc = sb("Wc", [VD // 2, 2, D])
    bb, alog, dtb = (sb(n, [P, H]) for n in ("bb", "alog", "dtb"))
    gn = sb("gn", [P, DV])
    ZPf = sb("ZP", [P, 2 * B * GPAD])
    ZP = ZPf[:, :].rearrange("p (i b t) -> p i b t", i=2, b=B)
    XS = sb("XS", [P, 2, NT * P])
    PR = sb("PR", [P, NT, W3])
    KP = sb("KP", [P, NT, 2, H, KP_])
    SQ = sb("SQ", [P, NT, VD])
    n2 = sb("n2", [P, NT, 2 * H])
    t1, t2, t3, t4, ld, beta = (sb(n, [P, NT, H]) for n in ("t1", "t2", "t3", "t4", "ld", "beta"))
    two = lambda n, sh: [sb(f"{n}{a}", sh) for a in range(2)]
    kq, kqT = two("kq", [P, 2, P]), two("kqT", [P, 2, P])
    X4 = two("X4", [P, 2, H, P])
    vg, ug = two("vg", [P, H, DV]), two("ug", [P, H, DV])
    ldg, beg = two("ldg", [P, H]), two("beg", [P, H])
    OA = ZPf[:, 0:NT * VD].rearrange("p (n c) -> p n c", c=VD)
    oT = [sb(f"oT{i}", [VD // 2, 2, P]) for i in range(2)]
    core = Core(k, "a4c", ctx, False)
    flat = lambda t: t[:, :, :].rearrange("p a b -> p (a b)")
    Gp, Qp, T1, Wb = core.PP[0][:, 0], core.PP[0][:, 1], core.T1[0], core.W[0]
    Sm = flat(core.W[1])
    QO, KO, VO, GO, AO = 0, KD, 2 * KD, 2 * KD + VD, 2 * KD + 2 * VD

    with nc.Block() as block:
        @block.sync
        def _(sp):
            sp.dma_start(Win[:, :, :].rearrange("p a c -> p (a c)"), d["L1_attn_W_in"]).then_inc(s["ldw"], 16)
            for i, n in enumerate(("x", "z")):
                sp.dma_start(cw[:, i, :], d[f"L1_attn_conv_{n}_w"].rearrange("c o j -> c (o j)")).then_inc(s["ldw"], 16)
                sp.dma_start(cb[:, i:i + 1], d[f"L1_attn_conv_{n}_b"].rearrange("(c o) -> c o", o=1)).then_inc(s["ldw"], 16)
            for o, w, n in ((QO, KD, "W_q"), (KO, KD, "W_k"), (VO, VD, "W_v"), (GO, VD, "W_g"), (AO, H, "W_gk"), (AO + H, H, "W_b")):
                sp.dma_start(Wp[:, o:o + w], d["L1_attn_" + n]).then_inc(s["ldw"], 16)
            sp.dma_start(Wso[:, :, :], d["L1_attn_W_so"].rearrange("(a r) m -> r a m", a=2)).then_inc(s["ldw"], 16)
            sp.dma_start(Wo[:, :, :], d["L1_attn_W_out"].rearrange("(a r) m -> r a m", a=2)).then_inc(s["ldw"], 16)
            for t, n in ((bb, "b_b"), (alog, "A_log"), (dtb, "dt_bias"), (gn, "g_norm_w")):
                sp.dma_start(t[:, :], d["L1_attn_" + n].partition_broadcast(P)).then_inc(s["ldw"], 16)

        @block.gpsimd
        def _(pool):
            norm_pool(k, pool, s["n"])
            pool.memset(ZP[:, :, :, 0:1], 0.0).then_inc(s["pz"], 1)
            pool.memset(ZP[:, :, :, T + 1:GPAD], 0.0).then_inc(s["pz"], 1)
            pool.memset(KP[:, :, :, :, :], 0.0).then_inc(s["kz"], 1)
            with pool.Fori(0, NT // 2) as i:
                core.parts(pool, s, i)
            pool.wait_ge(s["o1"], 3)
            pool.tensor_tensor(t1[:, :, :].rearrange("p n h -> p (n h)"), t1[:, :, :].rearrange("p n h -> p (n h)"),
                               k.half[:, 0:1].to_broadcast([P, NT * H]), ALU.pow).then_inc(s["o1s"], 1)

        @block.scalar
        def _(act):
            act.wait_ge(s["wt"], 1)
            act.activation(flat(WsoT), Sm[:, 0:VD], ACT.Copy).then_inc(s["wc"], 1)
            act.wait_ge(s["wf"], 1)
            act.activation(flat(Wc), Sm[0:VD // 2, 0:2 * D], ACT.Copy).then_inc(s["wfc"], 1)
            norm_scalar(k, act, s["n"], [flat(Gp), flat(Qp)])
            for g in range(8):
                i, c = g // 4, g % 4
                act.wait_ge(s["xz"], g + 1)
                act.activation(ZP[:, i, 8 * c:8 * c + 8, 1:T + 1], flat((T1, Wb)[g % 2]).rearrange("p (b t) -> p b t", t=T), ACT.Copy)\
                   .then_inc(s["xzc"], 1)
            for i in range(2):
                act.wait_ge(s[f"cv{i}"], 4)
                act.activation(XS[:, i, :], XS[:, i, :], ACT.Silu, bias=cb[:, i:i + 1]).then_inc(s[f"sl{i}"], 1)
            act.wait_ge(s["pjc"], 2 * NT)
            act.activation(PR[:, :, GO:GO + VD], PR[:, :, GO:GO + VD], ACT.Silu).then_inc(s["g3"], 1)
            act.wait_ge(s["l2"], 4)
            act.activation(n2[:, :, :], n2[:, :, :], ACT.Sqrt).then_inc(s["l2s"], 1)
            act.wait_ge(s["g1"], 3)
            act.activation(t2[:, :, :], t1[:, :, :], ACT.Abs).then_inc(s["g2"], 1)
            act.wait_ge(s["g2"], 1)
            act.activation(t2[:, :, :], t2[:, :, :], ACT.Exp, scale=-1.0).then_inc(s["g2"], 1)
            act.activation(beta[:, :, :], beta[:, :, :], ACT.Exp, scale=-1.0).then_inc(s["g3"], 1)
            act.activation(alog[:, :], alog[:, :], ACT.Exp).then_inc(s["g3"], 1)
            act.wait_ge(s["l2"], 6)
            def front(i):
                for a in range(2):
                    g = 2 * i + a
                    wait(act, s["kt"], g - 1)
                    act.activation(kq[a][:, :, :], KP[:, bass.ds(g, 1), :, :, :].rearrange("p o w h c -> p (o w) (h c)"), ACT.Copy).then_inc(s["cp"], 1)
                for a in range(2):
                    g = 2 * i + a
                    wait(act, s["kt"], g + 1)
                    wait(act, s["gq"], g - 1)
                    act.activation(kqT[a][:, :, :].rearrange("p w t -> p (w t)"), flat(core.W[a])[:, 0:2 * P], ACT.Copy).then_inc(s["ktc"], 1)

            def pair(i, more):
                for a in range(2):
                    g = 2 * i + a
                    wait(act, s["w4"], g - 1)
                    act.activation(vg[a][:, :, :], PR[:, bass.ds(g, 1), VO:VO + VD].rearrange("p o (h c) -> p (o h) c", c=DV), ACT.Copy)\
                       .then_inc(s["cv"], 1)
                core.copies(act, s, i, 1, 3)
                if more:
                    front(i + 1)
                core.copies(act, s, i, 3, LEVELS)
                if more:
                    core.decays(act, s, i + 1)

            front(0)
            core.decays(act, s, 0)
            with act.Fori(0, NT // 2 - 1) as i:
                pair(i, True)
            pair(NT // 2 - 1, False)
            for n in range(NT):
                act.wait_ge(s["ot"], n + 1)
                if n >= 2:
                    act.wait_ge(s["y"], n - 1)
                act.activation(oT[n % 2][:, :, :], (T1, Wb)[n % 2][0:VD // 2, 0:2, :], ACT.Copy).then_inc(s["otc"], 1)

        @block.vector
        def _(v):
            norm_vector(k, v, s["n"])
            v.wait_ge(s["ldw"], 16 * 17)
            for i in range(2):
                v.wait_ge(s["xzc"], 4 * i + 4)
                v.wait_ge(s["pz"], 2)
                out = XS[:, i, :].rearrange("p (b t) -> p b t", t=T)
                for j in range(4):
                    src = ZP[:, i, :, j:j + T]
                    if j == 0:
                        v.tensor_scalar(out, src, cw[:, i, 0:1], None, ALU.mult).then_inc(s[f"cv{i}"], 1)
                    else:
                        v.wait_ge(s[f"cv{i}"], j)
                        v.scalar_tensor_tensor(out=out, in0=src, scalar=cw[:, i, j:j + 1], in1=out, op0=ALU.mult, op1=ALU.add)\
                         .then_inc(s[f"cv{i}"], 1)
            for n in range(NT):
                v.wait_ge(s["pj"], n + 1)
                b0, b1 = ((flat(Gp), flat(Qp)), (flat(T1), flat(Wb)))[n % 2]
                v.tensor_copy(PR[:, n, 0:512], b0).then_inc(s["pjc"], 1)
                v.tensor_copy(PR[:, n, 512:W3], b1[:, 0:W3 - 512]).then_inc(s["pjc"], 1)
            v.wait_ge(s["pjc"], 2 * NT)
            v.tensor_tensor(t1[:, :, :], PR[:, :, AO:AO + H], dtb[:, :].unsqueeze(1).to_broadcast([P, NT, H]), ALU.add).then_inc(s["g1"], 1)
            v.tensor_tensor(beta[:, :, :], PR[:, :, AO + H:W3], bb[:, :].unsqueeze(1).to_broadcast([P, NT, H]), ALU.add).then_inc(s["g1"], 1)
            v.wait_ge(s["g1"], 2)
            v.tensor_scalar(t3[:, :, :], t1[:, :, :], 0.0, None, ALU.max).then_inc(s["g1"], 1)
            v.tensor_tensor(SQ[:, :, 0:2 * KD], PR[:, :, 0:2 * KD], PR[:, :, 0:2 * KD], ALU.mult).then_inc(s["l2"], 1)
            v.wait_ge(s["l2"], 1)
            v.tensor_reduce(n2[:, :, :], SQ[:, :, 0:2 * KD].rearrange("p n (h c) -> p n h c", c=DK), AXX, ALU.add).then_inc(s["l2"], 1)
            v.wait_ge(s["l2"], 2)
            v.tensor_scalar(n2[:, :, :], n2[:, :, :], 1e-6, None, ALU.add).then_inc(s["l2"], 1)
            v.wait_ge(s["l2"], 3)
            v.reciprocal(n2[:, :, :], n2[:, :, :]).then_inc(s["l2"], 1)
            v.wait_ge(s["l2s"], 1)
            v.wait_ge(s["kz"], 1)
            for w, o in ((0, KO), (1, QO)):
                v.tensor_tensor(KP[:, :, w, :, 0:DK], PR[:, :, o:o + KD].rearrange("p n (h c) -> p n h c", c=DK),
                                n2[:, :, o // DK:o // DK + H].unsqueeze(3).to_broadcast([P, NT, H, DK]), ALU.mult).then_inc(s["l2"], 1)
            v.wait_ge(s["g3"], 3)
            v.tensor_scalar(beta[:, :, :], beta[:, :, :], 1.0, None, ALU.add).then_inc(s["g4"], 1)
            v.wait_ge(s["g4"], 1)
            v.reciprocal(beta[:, :, :], beta[:, :, :]).then_inc(s["g4"], 1)
            v.wait_ge(s["g2"], 2)
            v.wait_ge(s["g1"], 3)
            softplus_vector(v, s["sp"], t2[:, :, :], t1[:, :, :], t4[:, :, :], t3[:, :, :])
            v.scalar_tensor_tensor(out=ld[:, :, :], in0=t3[:, :, :], scalar=-1.0,
                                   in1=alog[:, :].unsqueeze(1).to_broadcast([P, NT, H]), op0=ALU.mult, op1=ALU.mult).then_inc(s["g4"], 1)
            v.wait_ge(s["g4"], 3)
            def front(i):
                for a in range(2):
                    wait(v, s["ktc"], 2 * i + a + 1)
                    wait(v, s["gq"], 2 * i + a - 1)
                    for w in range(2):
                        v.tensor_tensor(X4[a][:, w, :, :], kqT[a][:, w, :].unsqueeze(1).to_broadcast([P, H, P]),
                                        k.quad[:, :].unsqueeze(2).to_broadcast([P, H, P]), ALU.mult).then_inc(s["kx"], 1)

            def spread(i):
                for a in range(2):
                    v.tensor_copy(ldg[a][:, :], ld[:, bass.ds(2 * i + a, 1), :].rearrange("p o h -> p (o h)")).then_inc(s["ll"], 1)
                wait(v, s["ll"], 2 * i + 2)
                core.spread(v, s, i, [t[:, :] for t in ldg])

            def pair(i, more):
                gs = [(a, 2 * i + a) for a in range(2)]
                for a, g in gs:
                    v.tensor_copy(beg[a][:, :], beta[:, bass.ds(g, 1), :].rearrange("p o h -> p (o h)")).then_inc(s["lb"], 1)
                wait(v, s["lb"], 2 * i + 2)
                core.vector(v, s, i, [t[:, :] for t in beg])
                core.levels(v, s, i, 1, 3)
                if more:
                    front(i + 1)
                core.levels(v, s, i, 3, LEVELS)
                if more:
                    spread(i + 1)
                for a, g in gs:
                    wait(v, s["w4"], g + 1)
                    v.tensor_tensor(ug[a][:, :, :], core.W[a][:, :, 0:DV], beg[a][:, :].unsqueeze(2).to_broadcast([P, H, DV]), ALU.mult).then_inc(s["u"], 1)
                for a, g in gs:
                    wait(v, s["oo"], g + 1)
                    v.tensor_copy(OA[:, bass.ds(g, 1), :].rearrange("p o (h c) -> p (o h) c", c=DV), core.W[a][:, :, 0:DV]).then_inc(s["oc"], 1)

            spread(0)
            front(0)
            with v.Fori(0, NT // 2 - 1) as i:
                pair(i, True)
            pair(NT // 2 - 1, False)
            wait(v, s["oc"], NT)
            heads = lambda t: t.rearrange("p n (h c) -> p n h c", c=DV)
            O4, S4 = heads(OA[:, :, :]), heads(SQ[:, :, :])
            v.tensor_tensor(SQ[:, :, :], OA[:, :, :], OA[:, :, :], ALU.mult).then_inc(s["o1"], 1)
            v.wait_ge(s["o1"], 1)
            v.tensor_reduce(t1[:, :, :], S4, AXX, ALU.add).then_inc(s["o1"], 1)
            v.wait_ge(s["o1"], 2)
            v.tensor_scalar(t1[:, :, :], t1[:, :, :], 1.0 / DV, LN_EPS, ALU.mult, ALU.add).then_inc(s["o1"], 1)
            v.tensor_tensor(S4, heads(PR[:, :, GO:GO + VD]), gn[:, :].unsqueeze(1).unsqueeze(1).to_broadcast([P, NT, H, DV]), ALU.mult)\
             .then_inc(s["o1"], 1)
            v.wait_ge(s["o1"], 4)
            v.tensor_tensor(OA[:, :, :], OA[:, :, :], SQ[:, :, :], ALU.mult).then_inc(s["o1"], 1)
            v.wait_ge(s["o1"], 5)
            v.wait_ge(s["o1s"], 1)
            v.tensor_tensor(O4, O4, t1[:, :, :].unsqueeze(3).to_broadcast([P, NT, H, DV]), ALU.mult).then_inc(s["o1"], 1)
            for n in range(NT):
                v.wait_ge(s["y"], n + 1)
                v.tensor_tensor(k.x[:, n, :], k.x[:, n, :], (Gp, Qp)[n % 2][:, 0, :], ALU.add).then_inc(s["x"], 1)
            v.wait_ge(s["x"], NT)

        @block.tensor
        def _(pe):
            pe.wait_ge(s["ldw"], 16 * 17)
            for i in range(2):
                mm = pe.transpose(Sm[:, 96 * i:96 * i + 96], Wso[:, i, :], k.ident[0:96, 0:96])
            mm.then_inc(s["wt"], 1)
            pe.wait_ge(s["wc"], 1)
            for i in range(2):
                mm = pe.matmul(Sm[0:96, D * i:D * i + D], WsoT[:, i, :], Wo[:, 0, :], start=True, stop=True)
            mm.then_inc(s["wf"], 1)
            norm_tensor(k, pe, s["n"], [flat(Gp), flat(Qp)])
            for g in range(8):
                i, c = g // 4, g % 4
                pe.wait_ge(s["n"]["copied"], c + 1)
                if g >= 2:
                    pe.wait_ge(s["xzc"], g - 1)
                pe.matmul(flat((T1, Wb)[g % 2]), Win[:, i, :], k.hT[:, 512 * c:512 * c + 512], start=True, stop=True).then_inc(s["xz"], 1)
            pe.wait_ge(s["sl0"], 1)
            pe.wait_ge(s["xzc"], 8)
            for n in range(NT):
                if n >= 2:
                    pe.wait_ge(s["pjc"], 2 * (n - 1))
                b0, b1 = ((flat(Gp), flat(Qp)), (flat(T1), flat(Wb)))[n % 2]
                xs = XS[:, 0, P * n:P * n + P]
                pe.matmul(b0, xs, Wp[:, 0:512], start=True, stop=True)
                pe.matmul(b1[:, 0:W3 - 512], xs, Wp[:, 512:W3], start=True, stop=True).then_inc(s["pj"], 1)
            pe.wait_ge(s["pjc"], 2 * NT)
            pe.wait_ge(s["wfc"], 1)
            def front(i):
                for a in range(2):
                    g = 2 * i + a
                    wait(pe, s["cp"], g + 1)
                    wait(pe, s["oc"], g - 3)
                    for w in range(2):
                        mm = pe.transpose(core.W[a][:, w, :], kq[a][:, w, :], k.ident[:, :])
                    mm.then_inc(s["kt"], 1)

            def pair(i, more):
                gs = [(a, 2 * i + a) for a in range(2)]
                for a, g in gs:
                    wait(pe, s["kx"], 4 * i + 2 * a + 2)
                    wait(pe, s["xx"], core.at(i - 1, a, LEVELS - 1))
                    for w in range(2):
                        mm = pe.matmul(core.PP[a][:, w, :, :], kqT[a][:, 0, :], X4[a][:, w, :, :], start=True, stop=True)
                    mm.then_inc(s["gq"], 1)
                core.solve(pe, s, i, 1, 3)
                if more:
                    front(i + 1)
                core.solve(pe, s, i, 3, LEVELS)
                for a, g in gs:
                    wait(pe, s["xx"], core.at(i, a, LEVELS - 1))
                    wait(pe, s["cv"], g + 1)
                    if more:
                        wait(pe, s["ktc"], g + 3)
                    for h in range(H):
                        mm = pe.matmul(core.W[a][:, h, 0:DV], core.XX[a][:, 1, h, :], vg[a][:, h, :], start=True, stop=True)
                    mm.then_inc(s["w4"], 1)
                if more:
                    core.sums(pe, s, i + 1)
                for a, g in gs:
                    wait(pe, s["u"], g + 1)
                    for h in range(H):
                        mm = pe.matmul(core.W[a][:, h, 0:DV], core.QL[a][:, h, :], ug[a][:, h, :], start=True, stop=True)
                    mm.then_inc(s["oo"], 1)

            core.sums(pe, s, 0)
            front(0)
            with pe.Fori(0, NT // 2 - 1) as i:
                pair(i, True)
            pair(NT // 2 - 1, False)
            pe.wait_ge(s["o1"], 6)
            wait(pe, s["oc"], NT)

            def turned(n):
                if n >= 2:
                    pe.wait_ge(s["otc"], n - 1)
                for i in range(2):
                    mm = pe.transpose((T1, Wb)[n % 2][0:96, i, :], OA[:, n, 96 * i:96 * i + 96], k.ident[:, :])
                mm.then_inc(s["ot"], 1)

            turned(0)
            pe.wait_ge(s["sl1"], 1)
            for n in range(NT):
                if n + 1 < NT:
                    turned(n + 1)
                pe.wait_ge(s["otc"], n + 1)
                if n >= 2:
                    pe.wait_ge(s["x"], n - 1)
                y = (Gp, Qp)[n % 2][:, 0, :]
                for i in range(2):
                    pe.matmul(y, oT[n % 2][:, i, :], Wc[:, i, :], start=(i == 0), stop=False)
                pe.matmul(y, XS[:, 1, P * n:P * n + P], Wo[:, 1, :], start=False, stop=True).then_inc(s["y"], 1)
    ctx.close()


def ffn1_sems(k):
    s = {n: k.sem("a5_" + n) for n in ROUTE_SEMS + ("st", "ldx", "ldw", "cm", "wt", "wc", "wk", "q", "qc", "v", "vc", "h", "xh")}
    for n in MOE_SEMS + ("kx", "qs", "vx", "sc", "dm", "dx", "ds", "ex", "su", "rc", "pn", "pt", "pv", "mo", "r1", "r2", "zt", "zc", "pr", "hx"):
        s[n] = k.counted("a5_" + n)
    for n in ("n", "n1", "n2"):
        s[n] = norm_sems(k, "a5" + n)
    return s


def stage_ffn1(k, s):
    nc, d = k.nc, k.dram
    H, DH, KVH, Q4 = 16, 8, 4, P // B
    KD = KVH * DH
    ctx = ExitStack()
    sb = lambda n, sh, dt=F32: k.sb("a5_" + n, sh, dt, ctx)
    g1, b1, g2, b2 = (sb(n, [P, D]) for n in ("g1", "b1", "g2", "b2"))
    Wqr = sb("Wqr", [P, D])
    Wkvr = sb("Wkvr", [2 * KD, D])
    Wpr = sb("Wpr", [P, D])
    Wpp = sb("Wpp", [P, 4, KVH, DH])
    WqT, WpT, WkT = (sb(n, [P, P]) for n in ("WqT", "WpT", "WkT"))
    WkvT = sb("WkvT", [P, 2 * KD])
    Wrr = sb("Wrr", [E8, D])
    WrT = sb("WrT", [P, E8])
    W1 = sb("W1", [P, E8, 2 * P])
    W2 = sb("W2", [P, 2 * E8, D])
    cmask = sb("cmask", [P, B])
    Y = sb("Y", [P, NT, D])
    QT, KT = sb("QT", [P, NT * P]), sb("KT", [P, NT * P])
    V = sb("V", [P, NT, KD])
    two = lambda n, sh: [sb(f"{n}{i}", sh) for i in range(2)]
    qs, kx, vx = two("qs", [P, P]), two("kx", [P, Q4, H, B]), two("vx", [P, Q4, KD])
    Sm, PT, Om = (two(n, [P, H, B]) for n in ("Sm", "PT", "Om"))
    mm_, R, R2, zs = two("mm", [P, H]), two("R", [P, 4 * B]), two("R2", [P, 4 * B]), two("zs", [P, P])
    m = Moe(k, "a5m", ctx, 2, lambda e, f: W1[:, e, P * f:P * f + P], lambda e, f: W2[:, 2 * e + f, :], ACT.Gelu_apprx_tanh)
    LG = k.ps("a5_L", [P, 512], F32, ctx)
    logits = LG[:, 0:NT * E8].rearrange("p (n e) -> p n e", e=E8)
    banks = [m.Dn[i][:, :, :].rearrange("p j d -> p (j d)") for i in range(2)]
    SB, OB = m.U[0:2], m.U[2:4]
    hb = lambda t: t[:, :].rearrange("p (h q) -> p h q", q=B)
    flat = lambda t: t[:, :, :].rearrange("p a b -> p (a b)")

    with nc.Block() as block:
        @block.sync
        def _(sp):
            sp.dma_start(d["out"].rearrange("b t d -> (b t) d").rearrange("(n p) d -> p n d", p=P), k.x[:, :, :]).then_inc(s["st"], 16)
            sp.wait_ge(s["st"], 16)
            by_token = d["out"].rearrange("b (n q) d -> q b n d", q=Q4)
            for q in range(Q4):
                sp.dma_start(k.x[B * q:B * q + B, :, :], by_token[q]).then_inc(s["ldx"], 16)
            for t, n in ((g1, "ln1_weight"), (b1, "ln1_bias"), (g2, "ln2_weight"), (b2, "ln2_bias")):
                sp.dma_start(t[:, :], d["L1_ffn_" + n].partition_broadcast(P)).then_inc(s["ldw"], 16)
            sp.dma_start(Wqr[:, :], d["L1_ffn_qkv_weight"][0:P, :]).then_inc(s["ldw"], 16)
            sp.dma_start(Wkvr[:, :], d["L1_ffn_qkv_weight"][P:P + 2 * KD, :]).then_inc(s["ldw"], 16)
            sp.dma_start(Wpr[:, :], d["L1_ffn_proj_weight"]).then_inc(s["ldw"], 16)
            sp.dma_start(Wrr[:, :], d["L1_ffn_router_weight"]).then_inc(s["ldw"], 16)
            sp.dma_start(W1[:, :, :], d["L1_ffn_moe_w1"].rearrange("e d f -> d e f")).then_inc(s["ldw"], 16)
            sp.dma_start(W2[:, :, :], d["L1_ffn_moe_w2"].rearrange("e (f p) d -> p (e f) d", p=P)).then_inc(s["ldw"], 16)

        @block.gpsimd
        def _(pool):
            pool.memset(cmask[:, :], 0.0).then_inc(s["cm"], 1)
            for q in range(Q4):
                pool.wait_ge(s["cm"], q + 1)
                pool.affine_select(out=cmask[B * q:B * q + B, :], in_=cmask[B * q:B * q + B, :], compare_op=ALU.is_ge,
                                   fill=MASKED, base=0, pattern=[[-1, B]], channel_multiplier=1).then_inc(s["cm"], 1)
            pool.wait_ge(s["cm"], Q4 + 1)
            norm_pool(k, pool, s["n"])
            norm_pool(k, pool, s["n1"])
            pool.wait_ge(s["qc"], NT // 2)
            pool.wait_ge(s["vc"], 1)
            with pool.Fori(0, NT // 2) as i:
                gs = [(0, 2 * i), (1, 2 * i + 1)]
                for a, g in gs:
                    wait(pool, s["sc"], g - 1)
                    pool.tensor_tensor(kx[a][:, :, :, :],
                                    KT[:, bass.ds(g * P, P)].rearrange("p (t k) -> p t k", k=B).unsqueeze(2).to_broadcast([P, Q4, H, B]),
                                    k.heads[:, :].unsqueeze(1).unsqueeze(3).to_broadcast([P, Q4, H, B]), ALU.mult).then_inc(s["kx"], 1)
                for a, g in gs:
                    wait(pool, s["pv"], g - 1)
                    pool.tensor_tensor(vx[a][:, :, :], V[:, bass.ds(g, 1), :].to_broadcast([P, Q4, KD]),
                                    k.quad[:, :].unsqueeze(2).to_broadcast([P, Q4, KD]), ALU.mult).then_inc(s["vx"], 1)
            norm_pool(k, pool, s["n2"])

        @block.scalar
        def _(act):
            act.wait_ge(s["wt"], 1)
            act.activation(WqT[:, :], LG[:, 0:P], ACT.Copy).then_inc(s["wc"], 1)
            act.activation(WpT[:, :], LG[:, P:2 * P], ACT.Copy).then_inc(s["wc"], 1)
            act.activation(WkvT[:, :], LG[:, 2 * P:2 * P + 2 * KD], ACT.Copy).then_inc(s["wc"], 1)
            act.activation(WrT[:, :], LG[:, 3 * P:3 * P + E8], ACT.Copy).then_inc(s["wc"], 1)
            norm_scalar(k, act, s["n1"], banks)
            for c in range(NT // 4):
                act.wait_ge(s["q"], 2 * c + 1)
                act.activation(QT[:, 512 * c:512 * c + 512], SB[c % 2][:, :], ACT.Copy, scale=DH ** -0.5).then_inc(s["qc"], 1)
                act.wait_ge(s["q"], 2 * c + 2)
                act.activation(KT[:, 512 * c:512 * c + 512], OB[c % 2][:, :], ACT.Copy).then_inc(s["qc"], 1)
            act.wait_ge(s["qc"], NT // 2)
            with act.Fori(0, NT // 2) as i:
                for a in range(2):
                    g = 2 * i + a
                    wait(act, s["sc"], g - 1)
                    act.activation(qs[a][:, :], QT[:, bass.ds(g * P, P)], ACT.Copy).then_inc(s["qs"], 1)
                for a in range(2):
                    wait(act, s["ds"], 2 * i + a + 1)
                    act.activation(Sm[a][:, :, :], Sm[a][:, :, :], ACT.Exp).then_inc(s["ex"], 1)
                for a in range(2):
                    g = 2 * i + a
                    wait(act, s["zt"], g + 1)
                    act.activation(zs[a][:, :], banks[a][:, 0:P], ACT.Copy).then_inc(s["zc"], 1)
            norm_scalar(k, act, s["n2"], banks)
            route_scalar(k, act, s, m)
            m.scalar(act, s)

        @block.vector
        def _(v):
            v.wait_ge(s["ldx"], 16 * Q4)
            norm_vector(k, v, s["n"])
            v.wait_ge(s["n"]["norm"], NT)
            v.wait_ge(s["ldw"], 16 * 10)
            v.tensor_copy(Wpp[:, :, :, :], Wpr[:, :].rearrange("p (k h d) -> p h k d", k=KVH, h=4)).then_inc(s["wk"], 1)
            norm_vector(k, v, s["n1"], k.hn, Y, g1, b1)
            v.wait_ge(s["wc"], 3)
            v.tensor_copy(WkT[:, :].rearrange("p (k r d) -> p k r d", k=KVH, r=4),
                          WkvT[:, 0:KD].rearrange("p (k d) -> p k d", d=DH).unsqueeze(2).to_broadcast([P, KVH, 4, DH])).then_inc(s["wk"], 1)
            v.wait_ge(s["v"], 1)
            v.tensor_copy(flat(V), LG[:, :]).then_inc(s["vc"], 1)
            v.wait_ge(s["qc"], NT // 2)
            v.wait_ge(s["vc"], 1)
            v.wait_ge(s["cm"], 5)
            with v.Fori(0, NT // 2) as i:
                gs = [(0, 2 * i), (1, 2 * i + 1)]
                for a, g in gs:
                    wait(v, s["sc"], g + 1)
                    v.tensor_tensor(Sm[a][:, :, :], hb(SB[a]), cmask[:, :].unsqueeze(1).to_broadcast([P, H, B]), ALU.add).then_inc(s["dm"], 1)
                for a, g in gs:
                    wait(v, s["dm"], g + 1)
                    v.tensor_reduce(mm_[a][:, :], Sm[a][:, :, :], AXX, ALU.max).then_inc(s["dx"], 1)
                for a, g in gs:
                    wait(v, s["dx"], g + 1)
                    v.tensor_tensor(Sm[a][:, :, :], Sm[a][:, :, :], mm_[a][:, :].unsqueeze(2).to_broadcast([P, H, B]), ALU.subtract)\
                     .then_inc(s["ds"], 1)
                for a, g in gs:
                    wait(v, s["ex"], g + 1)
                    v.tensor_reduce(mm_[a][:, :], Sm[a][:, :, :], AXX, ALU.add).then_inc(s["su"], 1)
                for a, g in gs:
                    wait(v, s["su"], g + 1)
                    v.reciprocal(mm_[a][:, :], mm_[a][:, :]).then_inc(s["rc"], 1)
                for a, g in gs:
                    wait(v, s["rc"], g + 1)
                    v.tensor_tensor(Sm[a][:, :, :], Sm[a][:, :, :], mm_[a][:, :].unsqueeze(2).to_broadcast([P, H, B]), ALU.mult)\
                     .then_inc(s["pn"], 1)
                for a, g in gs:
                    wait(v, s["pn"], g + 1)
                    v.transpose(flat(PT[a]), flat(Sm[a])).then_inc(s["pt"], 1)
                for a, g in gs:
                    wait(v, s["pv"], g + 1)
                    v.tensor_tensor(Om[a][:, :, :].rearrange("p (k h) q -> p k (h q)", k=KVH),
                                    OB[a][:, :].rearrange("p (k f) -> p k f", k=KVH),
                                    k.subhead[:, :].unsqueeze(2).to_broadcast([P, KVH, 4 * B]), ALU.mult).then_inc(s["mo"], 1)
                for a, g in gs:
                    wait(v, s["mo"], g + 1)
                    v.tensor_reduce(R[a][:, :], Om[a][:, :, :].rearrange("p (k h) q -> p (h q) k", k=KVH), AXX, ALU.add).then_inc(s["r1"], 1)
                for a, g in gs:
                    wait(v, s["r1"], g + 1)
                    v.transpose(R2[a][:, :], R[a][:, :]).then_inc(s["r2"], 1)
                for a, g in gs:
                    wait(v, s["pr"], g + 1)
                    v.tensor_tensor(k.hn[:, bass.ds(g, 1), :].rearrange("p o d -> p (o d)"), k.hn[:, bass.ds(g, 1), :].rearrange("p o d -> p (o d)"),
                                    banks[a][:, P:2 * P], ALU.add).then_inc(s["hx"], 1)
            wait(v, s["hx"], NT)
            v.tensor_tensor(k.x[:, :, :], k.x[:, :, :], k.hn[:, :, :], ALU.add).then_inc(s["xh"], 1)
            v.wait_ge(s["n1"]["turned"], NT // 4)
            norm_vector(k, v, s["n2"], k.hn, Y, g2, b2)
            route_vector(k, v, s, logits, None, m)
            v.wait_ge(s["xh"], 1)
            m.vector(v, s)

        @block.tensor
        def _(pe):
            pe.wait_ge(s["ldw"], 16 * 10)
            pe.wait_ge(s["wk"], 1)
            pe.transpose(LG[:, 0:P], Wqr[:, :], k.ident[:, :])
            pe.transpose(LG[:, P:2 * P], Wpp[:, :, :, :].rearrange("p h k d -> p (h k d)"), k.ident[:, :])
            pe.transpose(LG[:, 2 * P:2 * P + 2 * KD], Wkvr[:, :], k.ident[0:2 * KD, 0:2 * KD])
            pe.transpose(LG[:, 3 * P:3 * P + E8], Wrr[:, :], k.ident[0:E8, 0:E8]).then_inc(s["wt"], 1)
            norm_tensor(k, pe, s["n1"], banks, Y)
            pe.wait_ge(s["wc"], 4)
            pe.wait_ge(s["wk"], 2)
            for c in range(NT // 4):
                pe.wait_ge(s["n1"]["copied"], c + 1)
                if c >= 2:
                    pe.wait_ge(s["qc"], 2 * (c - 1))
                h = k.hT[:, 512 * c:512 * c + 512]
                pe.matmul(SB[c % 2][:, :], WqT[:, :], h, start=True, stop=True).then_inc(s["q"], 1)
                pe.matmul(OB[c % 2][:, :], WkT[:, :], h, start=True, stop=True).then_inc(s["q"], 1)
            for n in range(NT):
                mm = pe.matmul(LG[:, KD * n:KD * n + KD], k.hT[:, P * n:P * n + P], WkvT[:, KD:2 * KD], start=True, stop=True)
            mm.then_inc(s["v"], 1)
            pe.wait_ge(s["qc"], NT // 2)
            with pe.Fori(0, NT // 2) as i:
                gs = [(0, 2 * i), (1, 2 * i + 1)]
                for a, g in gs:
                    wait(pe, s["qs"], g + 1)
                    wait(pe, s["kx"], g + 1)
                    wait(pe, s["dm"], g - 1)
                    for t in range(Q4):
                        mm = pe.matmul(SB[a][B * t:B * t + B, :], qs[a][:, B * t:B * t + B], kx[a][:, t, :, :], start=True, stop=True)
                    mm.then_inc(s["sc"], 1)
                for a, g in gs:
                    wait(pe, s["pt"], g + 1)
                    wait(pe, s["vx"], g + 1)
                    wait(pe, s["mo"], g - 1)
                    for t in range(Q4):
                        mm = pe.matmul(OB[a][B * t:B * t + B, :], vx[a][:, t, :], PT[a][:, :, :], start=True, stop=True)
                    mm.then_inc(s["pv"], 1)
                for a, g in gs:
                    wait(pe, s["r2"], g + 1)
                    wait(pe, s["hx"], g - 1)
                    pe.transpose(banks[a][:, 0:P], R2[a][:, :], k.ident[:, :]).then_inc(s["zt"], 1)
                for a, g in gs:
                    wait(pe, s["zc"], g + 1)
                    pe.matmul(banks[a][:, P:2 * P], zs[a][:, :], WpT[:, :], start=True, stop=True).then_inc(s["pr"], 1)
            norm_tensor(k, pe, s["n2"], banks, Y)
            pe.wait_ge(s["n2"]["copied"], NT // 4)
            pe.wait_ge(s["vc"], 1)
            route_tensor(k, pe, s, logits, WrT)
            m.tensor(pe, s)
    ctx.close()


def store_sems(k):
    return {"stored": k.sem("stored")}


def stage_store(k, s):
    nc = k.nc
    with nc.Block() as block:
        @block.sync
        def _(sp):
            by_token = k.dram["out"].rearrange("b (n q) d -> q b n d", q=P // B)
            for q in range(P // B):
                sp.dma_start(by_token[q], k.x[B * q:B * q + B, :, :]).then_inc(s["stored"], 16)
            sp.wait_ge(s["stored"], 16 * (P // B))


def program(nc, dram):
    stages = [(setup_sems, stage_setup), (xattn0_sems, stage_xattn0), (delta0_sems, stage_delta0), (moe0_sems, stage_moe0),
              (xattn1_sems, stage_xattn1), (delta1_sems, stage_delta1), (ffn1_sems, stage_ffn1), (store_sems, stage_store)]
    with ExitStack() as ctx:
        k = Kernel(nc, ctx, dram)
        for sems, body in stages:
            k.run(sems, body)


INPUTS = [
    "x", "ctx_1024", "mask_BxS2_ik0",
    "L0_xattn_Wq", "L0_xattn_bq", "L0_xattn_Wk", "L0_xattn_bk", "L0_xattn_Wv", "L0_xattn_bv", "L0_xattn_Wo", "L0_xattn_bo",
    "L0_attn_W_write", "L0_attn_W_read", "L0_attn_W_alpha", "L0_attn_W_beta", "L0_attn_A_log", "L0_attn_dt_bias",
    "L0_ffn_router_w", "L0_ffn_router_b", "L0_ffn_expert_up", "L0_ffn_expert_down",
    "L1_xattn_Wq", "L1_xattn_Wkv", "L1_xattn_Wout", "L1_xattn_gm", "L1_xattn_bm", "L1_xattn_gl", "L1_xattn_bl",
    "L1_attn_W_in", "L1_attn_conv_x_w", "L1_attn_conv_x_b", "L1_attn_conv_z_w", "L1_attn_conv_z_b",
    "L1_attn_W_q", "L1_attn_W_k", "L1_attn_W_v", "L1_attn_W_g", "L1_attn_W_gk", "L1_attn_W_b", "L1_attn_b_b",
    "L1_attn_A_log", "L1_attn_dt_bias", "L1_attn_g_norm_w", "L1_attn_W_so", "L1_attn_W_out",
    "L1_ffn_ln1_weight", "L1_ffn_ln1_bias", "L1_ffn_ln2_weight", "L1_ffn_ln2_bias", "L1_ffn_qkv_weight",
    "L1_ffn_proj_weight", "L1_ffn_router_weight", "L1_ffn_moe_w1", "L1_ffn_moe_w2",
]


def kernel(**inputs):
    import numpy as np
    import concourse.bacc as bacc
    from concourse.bass_utils import run_bass_kernel_spmd

    nc = bacc.Bacc("TRN2", target_bir_lowering=False, num_devices=1)
    arrays, dram = {}, {}
    for name in INPUTS:
        a = np.ascontiguousarray(inputs[name])
        arrays[f"in_{name}_dram"] = a
        dram[name] = nc.dram_tensor(f"in_{name}_dram", a.shape, mybir.dt.from_np(a.dtype), kind="ExternalInput").ap()
    dram["out"] = nc.dram_tensor("out_0_dram", (B, T, D), F32, kind="ExternalOutput").ap()
    program(nc, dram)
    r = run_bass_kernel_spmd(nc, [arrays], core_ids=[0])
    return r.results[0]["out_0_dram"]
```
